# Optimizing a Trainium2 kernel written in Bass

```python
import numpy as np
import jax
import jax.numpy as jnp

def _softmax(x, axis=-1):
    return jax.nn.softmax(x, axis=axis)

def _gelu(x):
    return jax.nn.gelu(x, approximate=True)

def _silu(x):
    return jax.nn.silu(x)

def _sigmoid(x):
    return jax.nn.sigmoid(x)

def _layernorm(x, axis=-1, eps=1e-05):
    m = jnp.mean(x, axis=axis, keepdims=True)
    v = jnp.var(x, axis=axis, keepdims=True)
    return (x - m) / jnp.sqrt(v + eps)

def _scatter_add(tgt, idx, src, axis=0):
    return tgt.at[idx].add(src)

def _segment_sum(src, seg, n):
    return jax.ops.segment_sum(src, seg, n)
kernel_name = 'mk_flamingo_gated_d1_seqx_r8_66cfca'

def setup_inputs(seed: int=0):
    np.random.seed(seed)
    _w = jnp.asarray

    def _rec_inputs():
        import jax
        import jax.numpy as jnp
        _rk = jax.random.key(seed)
        x = 7.22e-05 + 1 * jax.random.normal(jax.random.fold_in(_rk, 1), (32, 64, 128), jnp.float32)
        _lenS = 64 - jax.random.randint(jax.random.fold_in(_rk, 7), (32,), 0, max(1, 64 // 4) + 1, jnp.int32)
        _lenS2 = 64 - jax.random.randint(jax.random.fold_in(_rk, 8), (32,), 0, max(1, 64 // 4) + 1, jnp.int32)
        _ctx_1024P = jax.random.normal(jax.random.fold_in(_rk, 11), (32, 16, 128), jnp.float32)
        _ctx_1024c = jax.random.dirichlet(jax.random.fold_in(_rk, 511), 0.3 * jnp.ones((16,), jnp.float32), (32, 64))
        _ctx_1024t = jnp.einsum('bsk,bkd->bsd', _ctx_1024c, _ctx_1024P)
        _ctx_1024t = _ctx_1024t * jax.lax.rsqrt(jnp.mean(jnp.square(_ctx_1024t)) + 1e-12) * 0.953939
        ctx_1024 = 4.13588e-05 + 0.999923 * (_ctx_1024t + 0.3 * jax.random.normal(jax.random.fold_in(_rk, 611), (32, 64, 128), jnp.float32))
        _g = jax.random.normal(jax.random.fold_in(_rk, 9001), (2, 1), jnp.float32)
        _g = jnp.sign(_g) * jnp.maximum(jnp.abs(_g), 1.0) + (_g == 0) * 1.0
        g_xattn = _g[0]
        g_ffn = _g[1]
        return (x, ctx_1024, g_xattn, g_ffn)
    x, ctx_1024, g_xattn, g_ffn = _rec_inputs()

    def _L0_xattn_setup():
        import jax, jax.numpy as jnp
        import numpy as np
        D_MODEL = 128
        NHEAD = 16
        HEAD_DIM = D_MODEL // NHEAD
        key = jax.random.key(seed)
        ks = jax.random.split(key, 11)
        B, S, D = (4, 256, D_MODEL)
        scale = 1.0 / np.sqrt(D)
        inp = {'q': jax.random.normal(ks[0], (B, S, D), jnp.float32), 'k': jax.random.normal(ks[1], (B, S, D), jnp.float32), 'v': jax.random.normal(ks[2], (B, S, D), jnp.float32), 'Wq': jax.random.normal(ks[3], (D, D), jnp.float32) * scale, 'bq': jnp.zeros((D,), jnp.float32), 'Wk': jax.random.normal(ks[4], (D, D), jnp.float32) * scale, 'bk': jnp.zeros((D,), jnp.float32), 'Wv': jax.random.normal(ks[5], (D, D), jnp.float32) * scale, 'bv': jnp.zeros((D,), jnp.float32), 'Wo': jax.random.normal(ks[6], (D, D), jnp.float32) * scale, 'bo': jnp.zeros((D,), jnp.float32)}
        return inp
    _L0_xattn_all = _L0_xattn_setup()
    _L0_xattn_in = {k: v for k, v in _L0_xattn_all.items() if k in ('Wq', 'bq', 'Wk', 'bk', 'Wv', 'bv', 'Wo', 'bo')}
    del _L0_xattn_all

    def _L0_ffn_setup():
        import jax, jax.numpy as jnp
        import numpy as np
        NUM_EXPERTS = 8
        TOP_K = 2

        def _swiglu(x, w1, w2, w3):
            return jax.nn.silu(x @ w1) * (x @ w3) @ w2
        key = jax.random.key(seed)
        ks = jax.random.split(key, 9)
        B, S, D, H, E = (1, 128, 128, 128, NUM_EXPERTS)
        std = 0.02
        return {'x': jax.random.normal(ks[0], (B, S, D), jnp.float32), 'router_w': jax.random.normal(ks[1], (D, E), jnp.float32) * std, 'expert_bias': jnp.zeros((E,), jnp.float32), 'w1': jax.random.normal(ks[2], (E, D, H), jnp.float32) * std, 'w2': jax.random.normal(ks[3], (E, H, D), jnp.float32) * std, 'w3': jax.random.normal(ks[4], (E, D, H), jnp.float32) * std, 'sw1': jax.random.normal(ks[5], (D, H), jnp.float32) * std, 'sw2': jax.random.normal(ks[6], (H, D), jnp.float32) * std, 'sw3': jax.random.normal(ks[7], (D, H), jnp.float32) * std}
    _L0_ffn_all = _L0_ffn_setup()
    _L0_ffn_in = {k: v for k, v in _L0_ffn_all.items() if k in ('router_w', 'expert_bias', 'w1', 'w2', 'w3', 'sw1', 'sw2', 'sw3')}
    del _L0_ffn_all
    return {'x': x, 'ctx_1024': ctx_1024, 'g_xattn': g_xattn, 'g_ffn': g_ffn, 'L0_xattn_Wq': _L0_xattn_in['Wq'], 'L0_xattn_bq': _L0_xattn_in['bq'], 'L0_xattn_Wk': _L0_xattn_in['Wk'], 'L0_xattn_bk': _L0_xattn_in['bk'], 'L0_xattn_Wv': _L0_xattn_in['Wv'], 'L0_xattn_bv': _L0_xattn_in['bv'], 'L0_xattn_Wo': _L0_xattn_in['Wo'], 'L0_xattn_bo': _L0_xattn_in['bo'], 'L0_ffn_router_w': _L0_ffn_in['router_w'], 'L0_ffn_expert_bias': _L0_ffn_in['expert_bias'], 'L0_ffn_w1': _L0_ffn_in['w1'], 'L0_ffn_w2': _L0_ffn_in['w2'], 'L0_ffn_w3': _L0_ffn_in['w3'], 'L0_ffn_sw1': _L0_ffn_in['sw1'], 'L0_ffn_sw2': _L0_ffn_in['sw2'], 'L0_ffn_sw3': _L0_ffn_in['sw3']}

def reference(x, ctx_1024, g_xattn, g_ffn, L0_xattn_Wq, L0_xattn_bq, L0_xattn_Wk, L0_xattn_bk, L0_xattn_Wv, L0_xattn_bv, L0_xattn_Wo, L0_xattn_bo, L0_ffn_router_w, L0_ffn_expert_bias, L0_ffn_w1, L0_ffn_w2, L0_ffn_w3, L0_ffn_sw1, L0_ffn_sw2, L0_ffn_sw3):
    import jax
    import jax.numpy as jnp

    def _L0_xattn_ref(q, k, v, Wq, bq, Wk, bk, Wv, bv, Wo, bo):
        import jax, jax.numpy as jnp
        import numpy as np
        D_MODEL = 128
        NHEAD = 16
        HEAD_DIM = D_MODEL // NHEAD
        B, S, D = q.shape
        H, Hd = (NHEAD, HEAD_DIM)
        qh = (q @ Wq.T + bq).reshape(B, S, H, Hd).transpose(0, 2, 1, 3)
        kh = (k @ Wk.T + bk).reshape(B, S, H, Hd).transpose(0, 2, 1, 3)
        vh = (v @ Wv.T + bv).reshape(B, S, H, Hd).transpose(0, 2, 1, 3)
        scores = jnp.einsum('bhqd,bhkd->bhqk', qh, kh) / jnp.sqrt(jnp.float32(Hd))
        attn = jax.nn.softmax(scores, axis=-1)
        out = jnp.einsum('bhqk,bhkd->bhqd', attn, vh)
        out = out.transpose(0, 2, 1, 3).reshape(B, S, D)
        return out @ Wo.T + bo

    def _L0_ffn_ref(x, router_w, expert_bias, w1, w2, w3, sw1, sw2, sw3):
        import jax, jax.numpy as jnp
        import numpy as np
        NUM_EXPERTS = 8
        TOP_K = 2

        def _swiglu(x, w1, w2, w3):
            return jax.nn.silu(x @ w1) * (x @ w3) @ w2
        B, S, D = x.shape
        E, K = (NUM_EXPERTS, TOP_K)
        N = B * S
        x_flat = x.reshape(N, D)
        logits = x_flat @ router_w
        scores = jax.nn.softmax(logits.astype(jnp.float32), axis=-1)
        _, sel = jax.lax.top_k(scores + expert_bias[None, :], K)
        top_scores = jnp.take_along_axis(scores, sel, axis=-1)
        flat_exp = sel.reshape(-1)
        order = jnp.argsort(flat_exp)
        exp_sorted = flat_exp[order]
        routed_input = x_flat[order // K]
        routed_output = jnp.zeros_like(routed_input)
        for e in range(E):
            mask = (exp_sorted == e)[:, None]
            y_e = _swiglu(routed_input, w1[e], w2[e], w3[e])
            routed_output = routed_output + jnp.where(mask, y_e, 0.0)
        unsorted = jnp.zeros((N * K, D), routed_output.dtype).at[order].set(routed_output)
        unsorted = unsorted.reshape(N, K, D)
        out_experts = jnp.einsum('nk,nkd->nd', top_scores, unsorted)
        shared_out = _swiglu(x_flat, sw1, sw2, sw3)
        return (shared_out + out_experts).reshape(B, S, D)
    x = x + jnp.tanh(g_xattn[0]) * _L0_xattn_ref(_layernorm(x, axis=-1), ctx_1024, ctx_1024, L0_xattn_Wq, L0_xattn_bq, L0_xattn_Wk, L0_xattn_bk, L0_xattn_Wv, L0_xattn_bv, L0_xattn_Wo, L0_xattn_bo)
    x = x + jnp.tanh(g_ffn[0]) * _L0_ffn_ref(_layernorm(x, axis=-1), L0_ffn_router_w, L0_ffn_expert_bias, L0_ffn_w1, L0_ffn_w2, L0_ffn_w3, L0_ffn_sw1, L0_ffn_sw2, L0_ffn_sw3)
    return x

_drawn_inputs = setup_inputs


def setup_inputs(seed=0):
    import zlib

    import numpy as np

    out = dict(_drawn_inputs(seed))
    spreads = {'L0_xattn_bq': (0.0, 0.439),
     'L0_xattn_bk': (0.0, 0.8),
     'L0_xattn_bv': (0.0, 0.1),
     'L0_xattn_bo': (0.0, 0.1),
     'L0_ffn_expert_bias': (0.0, 0.8)}
    factors = {'L0_ffn_router_w': 8.0,
     'L0_ffn_w1': 8.0,
     'L0_ffn_w2': 8.0,
     'L0_ffn_w3': 8.0,
     'L0_ffn_sw1': 8.0,
     'L0_ffn_sw2': 8.0,
     'L0_ffn_sw3': 8.0}
    for name, (base, spread) in spreads.items():
        noise = np.random.default_rng([zlib.crc32(name.encode()), seed]).standard_normal(out[name].shape)
        drawn = base * np.exp(spread * noise) if base else spread * noise
        out[name] = jnp.asarray(drawn.astype(out[name].dtype))
    for name, factor in factors.items():
        out[name] = (out[name] * factor).astype(out[name].dtype)
    return out
```

```python
from contextlib import ExitStack

import numpy as np

import concourse.bass as bass
from concourse import mybir

F32 = mybir.dt.float32
F32R = mybir.dt.float32r
I32 = mybir.dt.int32
ALU = mybir.AluOpType
ACT = mybir.ActivationFunctionType
AX_X = mybir.AxisListType.X

D = 128
HEADS, HD = 16, 8
SEQ = 64
CHUNK = 512
PAIRS = CHUNK // D
UNITS = 2 * PAIRS
UH = HEADS // 2
QUAD = 32
COLT = D // QUAD
EXPERTS = 8
ALL_E = EXPERTS + 1
EPS = 1e-5
SCALE = float(HD) ** -0.5
RSQRT_SEED = 1597463007.0
NEWTON = 3

C_ID, C_EYE, C_NEG, C_DEN, C_LOW, C_MASK = 0, 128, 160, 288, 352, 416
C_ALL = 418


def constants():
    c = np.zeros((D, C_ALL), np.float32)
    p = np.arange(D)
    c[:, C_ID:C_ID + D] = np.eye(D)
    c[p, C_EYE + p % QUAD] = 1.0
    for b in range(2):
        c[b * SEQ:b * SEQ + QUAD, C_NEG + b * SEQ:C_NEG + (b + 1) * SEQ] = -1.0
    den = c[:, C_DEN:C_DEN + 64].reshape(D, 2, 2, 2, HD)
    for b in range(2):
        for hh in range(2):
            den[b * SEQ:(b + 1) * SEQ, hh, hh, b, :] = 1.0
        c[b * SEQ:(b + 1) * SEQ, C_MASK + b] = 1.0
    low = c[:, C_LOW:C_LOW + 64].reshape(D, EXPERTS, EXPERTS)
    for e in range(EXPERTS):
        low[:, e, :e] = 1.0
    return c


def block_program(nc, x, ctx_t, consts, wq_t, wk_t, wv_t, wo_t, wo_b, cols, bo, gates,
                  router, ebias, w1, w2, w3, sw1, sw2, sw3, out):
    tokens = x.shape[0]
    NCH = tokens // CHUNK

    ctx = ExitStack()
    with ctx:
        def sb(name, shape, dt=F32):
            return ctx.enter_context(nc.sbuf_tensor(name, shape, dt))

        def bank(name):
            return ctx.enter_context(nc.psum_tensor(name, [D, 512], F32))

        def sem(name):
            return ctx.enter_context(nc.semaphore(name))

        cst = sb("cst", [D, C_ALL])
        wq = sb("wq", [D, D])
        wk = sb("wk", [D, D])
        wv = sb("wv", [D, D])
        wo = sb("wo", [D, D])
        wob = sb("wob", [D, 2, 2, D])
        col = sb("col", [D, 3])
        bo_row = sb("bo_row", [D, D])
        gate_in = sb("gate_in", [D, 2])
        rw = sb("rw", [D, EXPERTS])
        eb = sb("eb", [D, EXPERTS])
        W1 = sb("W1", [D, ALL_E, D])
        W2 = sb("W2", [D, ALL_E, D])
        W3 = sb("W3", [D, ALL_E, D])
        negr = sb("negr", [D, D], F32R)
        tg = sb("tg", [D, 2])
        bv_rep = sb("bv_rep", [D, D])
        bias_sum = sb("bias_sum", [D, D])
        bias_row = sb("bias_row", [D, D])
        ident = cst[:, C_ID:C_ID + D]
        eye = cst[:, C_EYE:C_EYE + QUAD]
        low = cst[:, C_LOW:C_LOW + 64]
        xc = sb("xc", [D, PAIRS, D])
        ctxT = sb("ctxT", [D, CHUNK])
        xn = sb("xn", [D, PAIRS, D])
        xnT = sb("xnT", [D, CHUNK])
        qT = sb("qT", [D, CHUNK])
        kT = sb("kT", [D, CHUNK])
        q_blk = sb("q_blk", [D, HEADS, CHUNK])
        v_w = sb("v_w", [D, PAIRS, HEADS, QUAD])
        xres = sb("xres", [D, PAIRS, D])
        m_part = sb("m_part", [D, 16])
        m_other = sb("m_other", [D, 16])
        m_all = sb("m_all", [D, 16])
        m_exp = sb("m_exp", [D, 2, 512], F32R)
        P = sb("P", [D, 2, HEADS, SEQ])
        rden = sb("rden", [D, D])
        U = sb("U", [D, D])
        x2 = sb("x2", [D, PAIRS, D])
        x2n = sb("x2n", [D, PAIRS, D])
        x2nT = sb("x2nT", [D, CHUNK])
        st = [sb(f"st{n}", [D, PAIRS, 6]) for n in range(2)]
        dm = [sb(f"dm{n}", [D, PAIRS]) for n in range(2)]
        sm = [sb(f"sm{n}", [D, PAIRS]) for n in range(2)]
        cv = [sb(f"cv{n}", [D, PAIRS]) for n in range(2)]
        mean = [sb(f"mean{n}", [D, PAIRS]) for n in range(2)]
        neg_half = [sb(f"neg_half{n}", [D, PAIRS]) for n in range(2)]
        var = [sb(f"var{n}", [D, PAIRS]) for n in range(2)]
        half = [sb(f"half{n}", [D, PAIRS]) for n in range(2)]
        rstd = [sb(f"rstd{n}", [D, PAIRS]) for n in range(2)]
        three_halves = sb("three_halves", [D, PAIRS])
        nwt = [sb(f"nwt{n}", [D, PAIRS]) for n in range(2)]
        lg = sb("lg", [D, PAIRS, EXPERTS])
        lmax = sb("lmax", [D, PAIRS])
        lexp = sb("lexp", [D, PAIRS, EXPERTS])
        lsum = sb("lsum", [D, PAIRS])
        score = sb("score", [D, PAIRS, EXPERTS])
        biased = sb("biased", [D, PAIRS, EXPERTS])
        above = sb("above", [D, PAIRS, EXPERTS, EXPERTS])
        level = sb("level", [D, PAIRS, EXPERTS, EXPERTS])
        rank = sb("rank", [D, PAIRS, EXPERTS])
        gate = sb("gate", [D, PAIRS, EXPERTS])
        th = sb("th", [D, CHUNK])
        sl = sb("sl", [D, CHUNK])
        h = sb("h", [D, 2, CHUNK])
        acc = sb("acc", [D, PAIRS, D])

        SC = [bank("SC0"), bank("SC1")]
        AV = bank("AV")
        M0 = bank("M0")
        M1 = bank("M1")
        A1, A3, Y = bank("A1"), bank("A3"), bank("Y")

        base_in = sem("base_in")
        moe_in = sem("moe_in")
        x_in = sem("x_in")
        ctx_in = sem("ctx_in")
        qblk_in = sem("qblk_in")
        acc_free = sem("acc_free")
        set_pool = sem("set_pool")
        three_ready = sem("three_ready")
        set_dve = sem("set_dve")
        tg_ready = sem("tg_ready")
        bias_mm = sem("bias_mm")
        bias_ready = sem("bias_ready")
        ln_step = [sem("ln1_step"), sem("ln2_step")]
        half_done = [sem("half1_done"), sem("half2_done")]
        seeded = [sem("seeded1"), sem("seeded2")]
        newton = [sem("newton1"), sem("newton2")]
        xn_ready = sem("xn_ready")
        xT_mm = sem("xT_mm")
        xT_ready = sem("xT_ready")
        k_mm = sem("k_mm")
        k_ready = sem("k_ready")
        v_mm = sem("v_mm")
        v_ready = sem("v_ready")
        q_mm = sem("q_mm")
        q_ready = sem("q_ready")
        xres_ready = sem("xres_ready")
        s_mm = sem("s_mm")
        part_ready = sem("part_ready")
        other_ready = sem("other_ready")
        m_ready = sem("m_ready")
        mexp_ready = sem("mexp_ready")
        shift_mm = sem("shift_mm")
        p_ready = sem("p_ready")
        av_mm = sem("av_mm")
        rden_ready = sem("rden_ready")
        u_ready = sem("u_ready")
        wo_mm = sem("wo_mm")
        x2_ready = sem("x2_ready")
        x2n_ready = sem("x2n_ready")
        x2T_mm = sem("x2T_mm")
        x2T_ready = sem("x2T_ready")
        rt_mm = sem("rt_mm")
        lg_ready = sem("lg_ready")
        ldiff_ready = sem("ldiff_ready")
        lexp_ready = sem("lexp_ready")
        gate_step = sem("gate_step")
        a1_mm = sem("a1_mm")
        a3_mm = sem("a3_mm")
        th_ready = sem("th_ready")
        sl_ready = sem("sl_ready")
        h_ready = sem("h_ready")
        y_mm = sem("y_mm")
        acc_done = sem("acc_done")

        BASE = 12 * 16
        LN_STEPS = PAIRS + 8
        NEWTON_STEPS = 4 * NEWTON
        GATE_STEPS = 12
        QB = 16 * HEADS

        def wait(eng, s, value):
            if not isinstance(value, int) or value > 0:
                eng.wait_ge(s, value)

        block = ctx.enter_context(nc.Block())

        @block.sync
        def _(sp):
            def load_chunk(n):
                wait(sp, v_mm, n)
                sp.dma_start(ctxT[:], ctx_t[:, bass.ts(n, CHUNK)]).then_inc(ctx_in, 16)
                wait(sp, xn_ready, n)
                wait(sp, xres_ready, n)
                sp.dma_start(xc[:], x[bass.ts(n, CHUNK), :].rearrange("(t p) d -> p t d", p=D))\
                    .then_inc(x_in, 16)

            def spread_q(n):
                sp.wait_ge(q_ready, n + 1)
                for hd in range(HEADS):
                    rows = slice(hd * HD, (hd + 1) * HD)
                    sp.dma_start(q_blk[rows, hd, :], qT[rows, :]).then_inc(qblk_in, 16)

            def store(n):
                sp.wait_ge(acc_done, ALL_E * (n + 1))
                sp.dma_start(out[bass.ts(n, CHUNK), :].rearrange("(t p) d -> p t d", p=D), acc[:])\
                    .then_inc(acc_free, 16)

            sp.sem_inc(acc_free, 16)
            load_chunk(0)
            for dst, src in ((cst, consts), (wk, wk_t), (wv, wv_t), (col, cols), (wq, wq_t),
                             (wo, wo_t), (rw, router)):
                sp.dma_start(dst[:], src).then_inc(base_in, 16)
            sp.dma_start(wob[:], wo_b.rearrange("p (a b n) -> p a b n", a=2, b=2)).then_inc(base_in, 16)
            sp.dma_start(bo_row[:], bo.rearrange("(a n) -> a n", a=1).to_broadcast([D, D])).then_inc(base_in, 16)
            sp.dma_start(eb[:], ebias.rearrange("(a n) -> a n", a=1).to_broadcast([D, EXPERTS])).then_inc(base_in, 16)
            for g in range(2):
                sp.dma_start(gate_in[:, g:g + 1], gates[g].rearrange("(a n) -> a n", a=1).to_broadcast([D, 1]))\
                    .then_inc(base_in, 16)
            sp.wait_ge(set_pool, 1)
            spread_q(0)
            load_chunk(1)
            for dst, many, one in ((W1, w1, sw1), (W3, w3, sw3), (W2, w2, sw2)):
                sp.dma_start(dst[:, 0:EXPERTS, :], many.rearrange("e p n -> p e n")).then_inc(moe_in, 16)
                sp.dma_start(dst[:, EXPERTS, :], one).then_inc(moe_in, 16)
            spread_q(1)

            def body(n):
                load_chunk(n + 2)
                spread_q(n + 2)
                store(n)

            with sp.Fori(0, NCH - 2) as n:
                body(n)
            store(NCH - 2)
            store(NCH - 1)
            sp.wait_ge(acc_free, 16 * (NCH + 1))

        @block.gpsimd
        def _(pool):
            def spread_max(n, u):
                pool.wait_ge(m_ready, UNITS * n + u + 1)
                wait(pool, shift_mm, UNITS * n + u - 1)
                pool.tensor_tensor(
                    m_exp[:, u % 2, :].rearrange("p (k c) -> p k c", c=QUAD),
                    eye.unsqueeze(1).to_broadcast([D, 16, QUAD]),
                    m_all[:, :].unsqueeze(2).to_broadcast([D, 16, QUAD]), ALU.mult)\
                    .then_inc(mexp_ready, 1)

            def rsqrt_steps(n, k):
                y, v, t, s = rstd[k], neg_half[k], nwt[k], newton[k]
                pool.wait_ge(seeded[k], n + 1)
                at = NEWTON_STEPS * n
                for step in range(NEWTON):
                    wait(pool, s, at)
                    pool.tensor_tensor(t[:], y[:], y[:], ALU.mult).then_inc(s, 1)
                    pool.wait_ge(s, at + 1)
                    pool.tensor_tensor(t[:], t[:], v[:], ALU.mult).then_inc(s, 1)
                    pool.wait_ge(s, at + 2)
                    pool.tensor_tensor(t[:], t[:], three_halves[:], ALU.add).then_inc(s, 1)
                    pool.wait_ge(s, at + 3)
                    pool.tensor_tensor(y[:], y[:], t[:], ALU.mult).then_inc(s, 1)
                    at = at + 4

            def residual(n):
                pool.wait_ge(x_in, 16 * (n + 1))
                wait(pool, x2_ready, PAIRS * n)
                pool.tensor_tensor(xres[:], xc[:], bias_row[:, :].unsqueeze(1).to_broadcast([D, PAIRS, D]),
                                   ALU.add).then_inc(xres_ready, 1)

            def attend(n, project_next):
                for u in range(UNITS):
                    spread_max(n, u)
                    if project_next and u == 5:
                        rsqrt_steps(n + 1, 0)
                if project_next:
                    residual(n + 1)
                rsqrt_steps(n, 1)

            pool.memset(three_halves[:], 1.5).then_inc(three_ready, 1)
            pool.memset(q_blk[:], 0.0).then_inc(set_pool, 1)
            pool.memset(v_w[:], 0.0).then_inc(set_pool, 1)
            pool.wait_ge(three_ready, 1)
            rsqrt_steps(0, 0)
            pool.wait_ge(bias_ready, 2)
            residual(0)
            attend(0, True)
            with pool.Fori(0, NCH - 2) as n:
                attend(n + 1, True)
            attend(NCH - 1, False)

        @block.scalar
        def _(act):
            def keys_out(n):
                act.wait_ge(k_mm, n + 1)
                act.activation(kT[:], M0[:], ACT.Identity, bias=col[:, 1:2]).then_inc(k_ready, 1)

            def xT_out(n):
                act.wait_ge(xT_mm, n + 1)
                act.activation(xnT[:], M0[:], ACT.Copy).then_inc(xT_ready, 1)

            def queries_out(n):
                act.wait_ge(q_mm, n + 1)
                wait(act, qblk_in, QB * n)
                act.activation(qT[:], M0[:], ACT.Identity, bias=col[:, 0:1]).then_inc(q_ready, 1)

            def probs(n, u):
                act.wait_ge(shift_mm, UNITS * n + u + 1)
                if u % 2 == 0:
                    wait(act, av_mm, PAIRS * n + u // 2 - 1)
                half_heads = P[:, (u // 2) % 2, (u % 2) * UH:(u % 2 + 1) * UH, :]
                act.activation(half_heads.rearrange("p a b -> p (a b)"), SC[u % 2][:], ACT.Exp, scale=SCALE)\
                    .then_inc(p_ready, 1)

            def tanh_half(n, e):
                act.wait_ge(a1_mm, ALL_E * n + e + 1)
                act.activation(th[:], A1[:], ACT.Tanh, scale=0.5).then_inc(th_ready, 1)

            def x2T_out(n):
                act.wait_ge(x2T_mm, n + 1)
                act.activation(x2nT[:], M1[:], ACT.Copy).then_inc(x2T_ready, 1)

            def router_exp(n):
                act.wait_ge(ldiff_ready, n + 1)
                act.activation(lexp[:], lg[:], ACT.Exp).then_inc(lexp_ready, 1)

            def project(n):
                keys_out(n)
                xT_out(n)
                queries_out(n)

            def attend(n, m, project_next):
                for u in range(UNITS):
                    if m is not None:
                        tanh_half(m, u)
                    if u:
                        probs(n, u - 1)
                if project_next:
                    keys_out(n + 1)
                probs(n, UNITS - 1)
                if m is not None:
                    tanh_half(m, EXPERTS)
                if project_next:
                    xT_out(n + 1)
                    queries_out(n + 1)
                x2T_out(n)
                router_exp(n)

            act.wait_ge(base_in, BASE)
            act.activation(tg[:], gate_in[:], ACT.Tanh).then_inc(tg_ready, 1)
            project(0)
            attend(0, None, True)
            with act.Fori(0, NCH - 2) as n:
                attend(n + 1, n, True)
            attend(NCH - 1, NCH - 2, False)
            for e in range(ALL_E):
                tanh_half(NCH - 1, e)

        @block.vector
        def _(dve):
            def norm_stats(n, k, src, t):
                dve.bn_stats(st[k][:, t, :], src[:, t, :]).then_inc(ln_step[k], 1)

            def norm_seed(n, k):
                s, at = ln_step[k], LN_STEPS * n + PAIRS
                even, odd = st[k][:, :, 0:3], st[k][:, :, 3:6]
                dve.wait_ge(s, at)
                dve.tensor_tensor(dm[k][:], even[:, :, 1], odd[:, :, 1], ALU.subtract).then_inc(s, 1)
                dve.tensor_tensor(sm[k][:], even[:, :, 1], odd[:, :, 1], ALU.add).then_inc(s, 1)
                dve.tensor_tensor(cv[k][:], even[:, :, 2], odd[:, :, 2], ALU.add).then_inc(s, 1)
                dve.wait_ge(s, at + 1)
                dve.scalar_tensor_tensor(out=dm[k][:], in0=dm[k][:], scalar=0.25, in1=dm[k][:],
                                         op0=ALU.mult, op1=ALU.mult).then_inc(s, 1)
                dve.wait_ge(s, at + 2)
                dve.tensor_scalar(mean[k][:], sm[k][:], 0.5, None, ALU.mult).then_inc(s, 1)
                dve.wait_ge(s, at + 3)
                dve.tensor_scalar(cv[k][:], cv[k][:], 1.0 / D, EPS, ALU.mult, ALU.add).then_inc(s, 1)
                dve.wait_ge(s, at + 6)
                wait(dve, newton[k], NEWTON_STEPS * n)
                dve.tensor_tensor(var[k][:], cv[k][:], dm[k][:], ALU.add).then_inc(s, 1)
                dve.wait_ge(s, at + 7)
                dve.tensor_scalar(neg_half[k][:], var[k][:], -0.5, None, ALU.mult).then_inc(s, 1)
                dve.tensor_scalar(half[k][:].bitcast(I32), var[k][:].bitcast(I32), 1, None,
                                  ALU.logical_shift_right).then_inc(half_done[k], 1)
                dve.wait_ge(half_done[k], n + 1)
                dve.wait_ge(s, at + 8)
                dve.tensor_scalar(rstd[k][:].bitcast(I32), half[k][:].bitcast(I32), -1.0, RSQRT_SEED,
                                  ALU.mult, ALU.add).then_inc(seeded[k], 1)

            def norm_apply(n, k, src, dst, done):
                dve.wait_ge(newton[k], NEWTON_STEPS * (n + 1))
                for t in range(PAIRS):
                    last = dve.tensor_scalar(dst[:, t, :], src[:, t, :], mean[k][:, t:t + 1], rstd[k][:, t:t + 1],
                                             ALU.subtract, ALU.mult)
                last.then_inc(done, 1)

            def x_stats(n):
                dve.wait_ge(x_in, 16 * (n + 1))
                for t in range(PAIRS):
                    norm_stats(n, 0, xc, t)
                norm_seed(n, 0)

            def x_norm(n):
                wait(dve, xT_mm, n)
                norm_apply(n, 0, xc, xn, xn_ready)

            def values_out(n):
                dve.wait_ge(v_mm, n + 1)
                src = M0[:].rearrange("p (k a d) -> p k a d", a=2, d=HD)
                for b in range(2):
                    flat = v_w[:].rearrange("p t (k a) c -> p (t k) (a c)", a=2)
                    for a in range(2):
                        at = a * (QUAD + 2 * HD) + b * HD
                        last = dve.tensor_scalar(flat[:, :, at:at + HD], src[:, :, a, :],
                                                 cst[:, C_MASK + b:C_MASK + b + 1], None, ALU.mult)
                last.then_inc(v_ready, 1)

            def unit_max(n, u):
                at = UNITS * n + u
                dve.wait_ge(s_mm, at + 1)
                wait(dve, m_ready, at)
                dve.tensor_reduce(m_part[:], SC[u % 2][:].rearrange("p (k c) -> p k c", c=QUAD), AX_X, ALU.max,
                                  apply_transpose=True).then_inc(part_ready, 1)
                dve.wait_ge(part_ready, at + 1)
                for b in range(2):
                    last = dve.tensor_copy(m_other[b * SEQ:b * SEQ + QUAD, :],
                                           m_part[b * SEQ + QUAD:(b + 1) * SEQ, :])
                last.then_inc(other_ready, 1)
                dve.wait_ge(other_ready, at + 1)
                wait(dve, mexp_ready, at)
                dve.tensor_tensor(m_all[:], m_part[:], m_other[:], ALU.max).then_inc(m_ready, 1)

            def normalise(n, t):
                at = PAIRS * n + t
                dve.wait_ge(av_mm, at + 1)
                wait(dve, u_ready, at)
                dve.reciprocal(rden[:], AV[:, D:2 * D]).then_inc(rden_ready, 1)
                dve.wait_ge(rden_ready, at + 1)
                wait(dve, wo_mm, at)
                dve.tensor_tensor(U[:], AV[:, 0:D], rden[:], ALU.mult).then_inc(u_ready, 1)

            def residual(n, m, t):
                at = PAIRS * n + t
                dve.wait_ge(wo_mm, at + 1)
                if t == 0:
                    dve.wait_ge(xres_ready, n + 1)
                    wait(dve, x2n_ready, n)
                    if m is not None:
                        dve.wait_ge(acc_done, ALL_E * m + 1)
                dve.scalar_tensor_tensor(out=x2[:, t, :], in0=M1[:, t * D:(t + 1) * D], scalar=tg[:, 0:1],
                                         in1=xres[:, t, :], op0=ALU.mult, op1=ALU.add).then_inc(x2_ready, 1)
                dve.wait_ge(x2_ready, at + 1)
                norm_stats(n, 1, x2, t)

            def gates_of(n):
                s, at = gate_step, GATE_STEPS * n
                k = [0]

                def step(ins):
                    k[0] += 1
                    ins.then_inc(s, 1)
                    dve.wait_ge(s, at + k[0])

                def over(a):
                    return a[:, :].unsqueeze(2).to_broadcast([D, PAIRS, EXPERTS])

                dve.wait_ge(rt_mm, n + 1)
                dve.tensor_copy(lg[:].rearrange("p t e -> p (t e)"), M1[:, 0:PAIRS * EXPERTS]).then_inc(lg_ready, 1)
                dve.wait_ge(lg_ready, n + 1)
                step(dve.tensor_reduce(lmax[:], lg[:], AX_X, ALU.max))
                dve.tensor_tensor(lg[:], lg[:], over(lmax), ALU.subtract).then_inc(ldiff_ready, 1)
                dve.wait_ge(lexp_ready, n + 1)
                step(dve.tensor_reduce(lsum[:], lexp[:], AX_X, ALU.add))
                step(dve.reciprocal(lsum[:], lsum[:]))
                step(dve.tensor_tensor(score[:], lexp[:], over(lsum), ALU.mult))
                step(dve.tensor_tensor(biased[:], score[:], eb[:, :].unsqueeze(1).to_broadcast([D, PAIRS, EXPERTS]),
                                       ALU.add))
                other = biased[:].unsqueeze(2).to_broadcast([D, PAIRS, EXPERTS, EXPERTS])
                pairwise = above[:].rearrange("p t e f -> p (t e) f")
                same = level[:].rearrange("p t e f -> p (t e) f")
                step(dve.tensor_tensor(above[:], other, by_expert(biased), ALU.is_gt))
                step(dve.tensor_tensor(level[:], other, by_expert(biased), ALU.is_ge))
                step(dve.tensor_tensor(level[:].rearrange("p t e f -> p t (e f)"),
                                       level[:].rearrange("p t e f -> p t (e f)"),
                                       low.unsqueeze(1).to_broadcast([D, PAIRS, EXPERTS * EXPERTS]), ALU.mult))
                step(dve.tensor_tensor(pairwise, pairwise, same, ALU.max))
                step(dve.tensor_reduce(rank[:].rearrange("p t e -> p (t e)"), pairwise, AX_X, ALU.add))
                step(dve.scalar_tensor_tensor(out=rank[:], in0=rank[:], scalar=1.5, in1=score[:],
                                              op0=ALU.is_lt, op1=ALU.mult))
                step(dve.tensor_scalar(gate[:], rank[:], tg[:, 1:2], None, ALU.mult))
                assert k[0] == GATE_STEPS

            def by_expert(a):
                return a[:].unsqueeze(3).to_broadcast([D, PAIRS, EXPERTS, EXPERTS])

            def silu(n, e):
                at = ALL_E * n + e
                dve.wait_ge(th_ready, at + 1)
                if e:
                    dve.wait_ge(h_ready, at)
                dve.scalar_tensor_tensor(out=sl[:], in0=th[:], scalar=1.0, in1=A1[:], op0=ALU.add, op1=ALU.mult)\
                    .then_inc(sl_ready, 1)

            def hidden(n, e):
                at = ALL_E * n + e
                dve.wait_ge(a3_mm, at + 1)
                dve.wait_ge(sl_ready, at + 1)
                if e > 1:
                    dve.wait_ge(y_mm, at - 1)
                dve.scalar_tensor_tensor(out=h[:, e % 2, :], in0=A3[:], scalar=0.5, in1=sl[:],
                                         op0=ALU.mult, op1=ALU.mult).then_inc(h_ready, 1)

            def accumulate(n, e):
                at = ALL_E * n + e
                dve.wait_ge(y_mm, at + 1)
                if e == 0:
                    dve.wait_ge(acc_free, 16 * (n + 1))
                else:
                    dve.wait_ge(acc_done, at)
                for t in range(PAIRS):
                    weight = gate[:, t, e:e + 1] if e < EXPERTS else tg[:, 1:2]
                    last = dve.scalar_tensor_tensor(out=acc[:, t, :], in0=Y[:, t * D:(t + 1) * D], scalar=weight,
                                                    in1=(acc if e else x2)[:, t, :], op0=ALU.mult, op1=ALU.add)
                last.then_inc(acc_done, 1)

            def attend(n, m, project_next):
                for u in range(UNITS):
                    unit_max(n, u)
                    if m is not None:
                        silu(m, u)
                        hidden(m, u)
                        if u:
                            accumulate(m, u - 1)
                    if project_next and u == 4:
                        x_stats(n + 1)
                    if u % 2 == 0 and u:
                        normalise(n, u // 2 - 1)
                    if u % 2 and u > 1:
                        residual(n, m, u // 2 - 1)
                    if project_next and u == 7:
                        x_norm(n + 1)
                if m is not None:
                    silu(m, EXPERTS)
                    accumulate(m, EXPERTS - 1)
                normalise(n, PAIRS - 1)
                if m is not None:
                    hidden(m, EXPERTS)
                if project_next:
                    values_out(n + 1)
                residual(n, m, PAIRS - 1)
                norm_seed(n, 1)
                wait(dve, x2T_mm, n)
                if m is not None:
                    accumulate(m, EXPERTS)
                norm_apply(n, 1, x2, x2n, x2n_ready)
                gates_of(n)

            dve.memset(m_other[:], 0.0).then_inc(set_dve, 1)
            dve.wait_ge(base_in, BASE)
            dve.tensor_copy(negr[:], cst[:, C_NEG:C_NEG + D]).then_inc(set_dve, 1)
            dve.memset(bv_rep[:], 0.0).then_inc(set_dve, 1)
            dve.wait_ge(set_dve, 3)
            dve.tensor_scalar(bv_rep[:], bv_rep[:], col[:, 2:3], None, ALU.add).then_inc(set_dve, 1)
            x_stats(0)
            dve.wait_ge(bias_mm, 1)
            dve.tensor_tensor(bias_sum[:], M1[:, 0:D], bo_row[:], ALU.add).then_inc(bias_ready, 1)
            dve.wait_ge(bias_ready, 1)
            dve.wait_ge(tg_ready, 1)
            dve.tensor_scalar(bias_row[:], bias_sum[:], tg[:, 0:1], None, ALU.mult).then_inc(bias_ready, 1)
            x_norm(0)
            dve.wait_ge(set_pool, 2)
            values_out(0)
            attend(0, None, True)
            with dve.Fori(0, NCH - 2) as n:
                attend(n + 1, n, True)
            attend(NCH - 1, NCH - 2, False)
            for e in range(ALL_E):
                silu(NCH - 1, e)
                hidden(NCH - 1, e)
                if e:
                    accumulate(NCH - 1, e - 1)
            accumulate(NCH - 1, EXPERTS)

        @block.tensor
        def _(pe):
            def keys(n):
                pe.wait_ge(ctx_in, 16 * (n + 1))
                wait(pe, q_ready, n)
                pe.matmul(M0[:], wk[:], ctxT[:], start=True, stop=True).then_inc(k_mm, 1)

            def values(n):
                pe.wait_ge(k_ready, n + 1)
                for t in range(PAIRS):
                    last = pe.matmul(M0[:, t * D:(t + 1) * D], ctxT[:, t * D:(t + 1) * D], wv[:],
                                     start=True, stop=True)
                last.then_inc(v_mm, 1)

            def turn_x(n):
                pe.wait_ge(v_ready, n + 1)
                pe.wait_ge(xn_ready, n + 1)
                for t in range(PAIRS):
                    last = pe.transpose(M0[:, t * D:(t + 1) * D], xn[:, t, :], ident)
                last.then_inc(xT_mm, 1)

            def queries(n):
                pe.wait_ge(xT_ready, n + 1)
                pe.matmul(M0[:], wq[:], xnT[:], start=True, stop=True).then_inc(q_mm, 1)

            def scores(n, u):
                if u == 0:
                    pe.wait_ge(k_ready, n + 1)
                    pe.wait_ge(qblk_in, QB * (n + 1))
                wait(pe, p_ready, UNITS * n + u - 1)
                t, hs = u // 2, (u % 2) * UH
                for b in range(2):
                    tok = slice(t * D + b * SEQ, t * D + (b + 1) * SEQ)
                    last = pe.matmul(SC[u % 2][b * SEQ:(b + 1) * SEQ, :], kT[:, tok], q_blk[:, hs:hs + UH, tok],
                                     start=True, stop=False, skip_group_check=True)
                last.then_inc(s_mm, 1)

            def shift(n, u):
                pe.wait_ge(mexp_ready, UNITS * n + u + 1)
                pe.matmul(SC[u % 2][:], negr[:], m_exp[:, u % 2, :], start=False, stop=True,
                          skip_group_check=True).then_inc(shift_mm, 1)

            def attention(n, t):
                pe.wait_ge(p_ready, UNITS * n + 2 * t + 2)
                pe.wait_ge(v_ready, n + 1)
                wait(pe, u_ready, PAIRS * n + t)
                for r in range(2):
                    for a in range(2):
                        for j in range(COLT):
                            hd = 4 * j + 2 * r + a
                            pe.matmul(AV[j * QUAD:(j + 1) * QUAD, r * SEQ:(r + 1) * SEQ], v_w[:, t, hd, :],
                                      P[:, t % 2, hd, :], start=(a == 0), stop=(a == 1), skip_group_check=True)
                for a in range(2):
                    for j in range(COLT):
                        den = cst[:, C_DEN + a * QUAD:C_DEN + (a + 1) * QUAD]
                        last = pe.matmul(AV[j * QUAD:(j + 1) * QUAD, D:2 * D], den,
                                         P[:, t % 2, 4 * j + a:4 * j + a + 3:2, :], start=(a == 0), stop=(a == 1),
                                         skip_group_check=True)
                last.then_inc(av_mm, 1)

            def project_out(n, t):
                at = PAIRS * n + t
                pe.wait_ge(u_ready, at + 1)
                if t == 0:
                    wait(pe, lg_ready, n)
                else:
                    pe.wait_ge(x2_ready, at)
                for r in range(2):
                    for b in range(2):
                        last = pe.matmul(M1[b * SEQ:(b + 1) * SEQ, t * D:(t + 1) * D], U[:, r * SEQ:(r + 1) * SEQ],
                                         wob[:, r, b, :], start=(r == 0), stop=(r == 1), skip_group_check=True)
                last.then_inc(wo_mm, 1)

            def turn_x2(n):
                pe.wait_ge(x2n_ready, n + 1)
                for t in range(PAIRS):
                    last = pe.transpose(M1[:, t * D:(t + 1) * D], x2n[:, t, :], ident)
                last.then_inc(x2T_mm, 1)

            def route(n):
                pe.wait_ge(x2T_ready, n + 1)
                for t in range(PAIRS):
                    last = pe.matmul(M1[:, t * EXPERTS:(t + 1) * EXPERTS], x2nT[:, t * D:(t + 1) * D], rw[:],
                                     start=True, stop=True)
                last.then_inc(rt_mm, 1)

            def up1(n, e):
                if e == 0:
                    pe.wait_ge(x2T_ready, n + 1)
                if e:
                    pe.wait_ge(sl_ready, ALL_E * n + e)
                pe.matmul(A1[:], W1[:, e, :], x2nT[:], start=True, stop=True).then_inc(a1_mm, 1)

            def up3(n, e):
                if e:
                    pe.wait_ge(h_ready, ALL_E * n + e)
                pe.matmul(A3[:], W3[:, e, :], x2nT[:], start=True, stop=True).then_inc(a3_mm, 1)

            def down(n, e):
                pe.wait_ge(h_ready, ALL_E * n + e + 1)
                if e:
                    pe.wait_ge(acc_done, ALL_E * n + e)
                for t in range(PAIRS):
                    last = pe.matmul(Y[:, t * D:(t + 1) * D], h[:, e % 2, t * D:(t + 1) * D], W2[:, e, :],
                                     start=True, stop=True)
                last.then_inc(y_mm, 1)

            def attend(n, m, project_next):
                for u in range(UNITS):
                    scores(n, u)
                    if m is not None:
                        up1(m, u)
                    if u:
                        shift(n, u - 1)
                    if m is not None:
                        up3(m, u)
                        if u:
                            down(m, u - 1)
                    if u % 2 == 0 and u:
                        attention(n, u // 2 - 1)
                    if u % 2 and u > 1:
                        project_out(n, u // 2 - 1)
                if project_next:
                    keys(n + 1)
                shift(n, UNITS - 1)
                if m is not None:
                    up1(m, EXPERTS)
                    down(m, EXPERTS - 1)
                attention(n, PAIRS - 1)
                if m is not None:
                    up3(m, EXPERTS)
                if project_next:
                    values(n + 1)
                    turn_x(n + 1)
                project_out(n, PAIRS - 1)
                if project_next:
                    queries(n + 1)
                if m is not None:
                    down(m, EXPERTS)
                turn_x2(n)
                route(n)

            pe.wait_ge(base_in, BASE)
            pe.wait_ge(set_dve, 4)
            pe.matmul(M1[:, 0:D], bv_rep[:], wo[:], start=True, stop=True).then_inc(bias_mm, 1)
            keys(0)
            values(0)
            turn_x(0)
            queries(0)
            pe.wait_ge(bias_ready, 1)
            attend(0, None, True)
            pe.wait_ge(moe_in, 6 * 16)
            with pe.Fori(0, NCH - 2) as n:
                attend(n + 1, n, True)
            attend(NCH - 1, NCH - 2, False)
            for e in range(ALL_E):
                up1(NCH - 1, e)
                up3(NCH - 1, e)
                if e:
                    down(NCH - 1, e - 1)
            down(NCH - 1, EXPERTS)


def kernel(x, ctx_1024, g_xattn, g_ffn, L0_xattn_Wq, L0_xattn_bq, L0_xattn_Wk, L0_xattn_bk, L0_xattn_Wv,
           L0_xattn_bv, L0_xattn_Wo, L0_xattn_bo, L0_ffn_router_w, L0_ffn_expert_bias, L0_ffn_w1, L0_ffn_w2,
           L0_ffn_w3, L0_ffn_sw1, L0_ffn_sw2, L0_ffn_sw3):
    import concourse.bacc as bacc
    from concourse.bass_utils import run_bass_kernel_spmd

    def arr(a):
        return np.ascontiguousarray(np.asarray(a))

    B, S, _ = x.shape
    woT = arr(L0_xattn_Wo).T
    wo_b = np.zeros((COLT, 2, 2, HD, 2, 2, D), woT.dtype)
    by_head = woT.reshape(COLT, 2, 2, HD, D)
    for b in range(2):
        wo_b[:, :, b, :, :, b, :] = by_head.transpose(0, 2, 3, 1, 4)
    ins = {
        "x": arr(x).reshape(B * S, D),
        "ctx_t": arr(arr(ctx_1024).reshape(B * S, D).T),
        "consts": constants(),
        "wq_t": arr(arr(L0_xattn_Wq).T), "wk_t": arr(arr(L0_xattn_Wk).T), "wv_t": arr(arr(L0_xattn_Wv).T),
        "wo_t": arr(woT), "wo_b": wo_b.reshape(D, 4 * D),
        "cols": arr(np.stack([arr(L0_xattn_bq), arr(L0_xattn_bk), arr(L0_xattn_bv)], axis=1)),
        "bo": arr(L0_xattn_bo), "gates": arr(np.stack([arr(g_xattn), arr(g_ffn)])),
        "router": arr(L0_ffn_router_w), "ebias": arr(L0_ffn_expert_bias),
        "w1": arr(L0_ffn_w1), "w2": arr(L0_ffn_w2), "w3": arr(L0_ffn_w3),
        "sw1": arr(L0_ffn_sw1), "sw2": arr(L0_ffn_sw2), "sw3": arr(L0_ffn_sw3),
    }
    nc = bacc.Bacc("TRN2", target_bir_lowering=False, num_devices=1)
    aps = {n: nc.dram_tensor("in_" + n, a.shape, mybir.dt.from_np(a.dtype), kind="ExternalInput").ap()
           for n, a in ins.items()}
    out = nc.dram_tensor("out_y", (B * S, D), F32, kind="ExternalOutput").ap()
    block_program(nc, **aps, out=out)
    r = run_bass_kernel_spmd(nc, [{"in_" + n: a for n, a in ins.items()}], core_ids=[0])
    return r.results[0]["out_y"].reshape(B, S, D)
```

```python
from contextlib import ExitStack

import numpy as np

import concourse.bass as bass
from concourse import mybir

F32 = mybir.dt.float32
F32R = mybir.dt.float32r
I32 = mybir.dt.int32
ALU = mybir.AluOpType
ACT = mybir.ActivationFunctionType
AX_X = mybir.AxisListType.X

D = 128
HEADS, HD = 16, 8
SEQ = 64
CHUNK = 512
PAIRS = CHUNK // D
UNITS = 2 * PAIRS
HALF = CHUNK // 2
UH = HEADS // 2
QUAD = 32
COLT = D // QUAD
EXPERTS = 8
ALL_E = EXPERTS + 1
EPS = 1e-5
SCALE = float(HD) ** -0.5
RSQRT_SEED = 1597463007.0
NEWTON = 3

C_ID, C_EYE, C_NEG, C_DEN, C_LOW, C_MASK, C_HEAD = 0, 128, 160, 288, 352, 416, 418
C_ALL = 434


def constants():
    c = np.zeros((D, C_ALL), np.float32)
    p = np.arange(D)
    c[:, C_ID:C_ID + D] = np.eye(D)
    c[p, C_EYE + p % QUAD] = 1.0
    for b in range(2):
        c[b * SEQ:b * SEQ + QUAD, C_NEG + b * SEQ:C_NEG + (b + 1) * SEQ] = -1.0
    den = c[:, C_DEN:C_DEN + 64].reshape(D, 2, 2, 2, HD)
    for b in range(2):
        for hh in range(2):
            den[b * SEQ:(b + 1) * SEQ, hh, hh, b, :] = 1.0
        c[b * SEQ:(b + 1) * SEQ, C_MASK + b] = 1.0
    c[p, C_HEAD + p // HD] = 1.0
    low = c[:, C_LOW:C_LOW + 64].reshape(D, EXPERTS, EXPERTS)
    for e in range(EXPERTS):
        low[:, e, :e] = 1.0
    return c


def block_program(nc, x, ctx_t, proj_w, rest_w, rows, w1, w2, w3, out):
    tokens = x.shape[0]
    NCH = tokens // CHUNK

    ctx = ExitStack()
    with ctx:
        def sb(name, shape, dt=F32):
            return ctx.enter_context(nc.sbuf_tensor(name, shape, dt))

        def bank(name):
            return ctx.enter_context(nc.psum_tensor(name, [D, 512], F32))

        def sem(name):
            return ctx.enter_context(nc.semaphore(name))

        proj_in = sb("proj_in", [D, proj_w.shape[1]])
        wk, wv, wq = (proj_in[:, k * D:(k + 1) * D] for k in range(3))
        col = proj_in[:, 3 * D:3 * D + 3]
        rest_in = sb("rest_in", [D, rest_w.shape[1]])
        cst = rest_in[:, 0:C_ALL]
        wo = rest_in[:, C_ALL:C_ALL + D]
        wob = rest_in[:, C_ALL + D:C_ALL + 5 * D].rearrange("p (a b n) -> p a b n", a=2, b=2)
        rw = rest_in[:, C_ALL + 5 * D:C_ALL + 5 * D + EXPERTS]
        rows_in = sb("rows_in", [D, rows.shape[0]])
        bo_row = rows_in[:, 0:D]
        eb = rows_in[:, D:D + EXPERTS]
        gate_in = rows_in[:, D + EXPERTS:D + EXPERTS + 2]
        W1 = sb("W1", [D, ALL_E, D])
        W2 = sb("W2", [D, ALL_E, D])
        W3 = sb("W3", [D, ALL_E, D])
        W1h, W1l, W3h, W3l = (sb(n, [D, ALL_E, D], F32R) for n in ("W1h", "W1l", "W3h", "W3l"))
        rwhl = sb("rwhl", [D, 2 * EXPERTS], F32R)
        rwh, rwl = rwhl[:, 0:EXPERTS], rwhl[:, EXPERTS:2 * EXPERTS]
        negr = sb("negr", [D, D], F32R)
        tg = sb("tg", [D, 2])
        bv_rep = sb("bv_rep", [D, D])
        bias_sum = sb("bias_sum", [D, D])
        bias_row = sb("bias_row", [D, D])
        ident = cst[:, C_ID:C_ID + D]
        eye = cst[:, C_EYE:C_EYE + QUAD]
        low = cst[:, C_LOW:C_LOW + 64]
        xc = sb("xc", [D, PAIRS, D])
        xr = sb("xr", [D, PAIRS, D])
        ctxT = sb("ctxT", [D, CHUNK])
        xn = sb("xn", [D, PAIRS, D])
        xnT = sb("xnT", [D, CHUNK])
        qT = sb("qT", [D, CHUNK])
        kT = sb("kT", [D, CHUNK])
        q_blk = sb("q_blk", [D, HEADS, CHUNK])
        v_w = sb("v_w", [D, PAIRS, HEADS, QUAD])
        xres = sb("xres", [D, PAIRS, D])
        m_part = sb("m_part", [D, 16])
        m_other = sb("m_other", [D, 16])
        m_all = sb("m_all", [D, 16])
        m_exp = sb("m_exp", [D, 2, 512], F32R)
        P = sb("P", [D, 2, HEADS, SEQ])
        rden = sb("rden", [D, D])
        U = sb("U", [D, D])
        x2 = sb("x2", [D, PAIRS, D])
        x2n = sb("x2n", [D, PAIRS, D])
        x2h, x2l = sb("x2h", [D, CHUNK], F32R), sb("x2l", [D, CHUNK], F32R)
        st = [sb(f"st{n}", [D, PAIRS, 6]) for n in range(2)]
        dm = [sb(f"dm{n}", [D, PAIRS]) for n in range(2)]
        sm = [sb(f"sm{n}", [D, PAIRS]) for n in range(2)]
        cv = [sb(f"cv{n}", [D, PAIRS]) for n in range(2)]
        mean = [sb(f"mean{n}", [D, PAIRS]) for n in range(2)]
        neg_half = [sb(f"neg_half{n}", [D, PAIRS]) for n in range(2)]
        var = [sb(f"var{n}", [D, PAIRS]) for n in range(2)]
        half = [sb(f"half{n}", [D, PAIRS]) for n in range(2)]
        rstd = [sb(f"rstd{n}", [D, PAIRS]) for n in range(2)]
        three_halves = sb("three_halves", [D, PAIRS])
        nwt = [sb(f"nwt{n}", [D, PAIRS]) for n in range(2)]
        lg = sb("lg", [D, PAIRS, EXPERTS])
        lmax = sb("lmax", [D, PAIRS])
        lexp = sb("lexp", [D, PAIRS, EXPERTS])
        lsum = sb("lsum", [D, PAIRS])
        score = sb("score", [D, PAIRS, EXPERTS])
        biased = sb("biased", [D, PAIRS, EXPERTS])
        above = sb("above", [D, PAIRS, EXPERTS, EXPERTS])
        level = sb("level", [D, PAIRS, EXPERTS, EXPERTS])
        rank = sb("rank", [D, PAIRS, EXPERTS])
        gate = sb("gate", [D, PAIRS, EXPERTS])
        th = sb("th", [D, 2, CHUNK])
        sl = sb("sl", [D, CHUNK])
        h = sb("h", [D, 2, CHUNK])
        x2_kept = sb("x2_kept", [D, PAIRS, D])
        ys = sb("ys", [D, 2, PAIRS, D])
        acc = sb("acc", [D, PAIRS, D])

        SC = [bank("SC0"), bank("SC1")]
        AV = bank("AV")
        M0 = bank("M0")
        M1 = bank("M1")
        A1, A3, Y = bank("A1"), bank("A3"), bank("Y")
        A1s, A3s, Ys = (A1, SC[0]), (A3, SC[1]), (Y, AV)

        SC_FIRST = (SC[0], SC[1], A1, Y)

        def is_first(n):
            return isinstance(n, int) and n == 0

        def is_last(n):
            return isinstance(n, int) and n == NCH - 1

        def score_bank(n, u):
            return SC_FIRST[u % 4] if is_first(n) else SC[u % 2]

        def two_banks(n, e):
            return e % 2 if is_last(n) else 0

        proj_loaded = sem("proj_loaded")
        rest_loaded = sem("rest_loaded")
        up_in = sem("up_in")
        down_in = sem("down_in")
        split_hi = sem("split_hi")
        split_lo = sem("split_lo")
        rw_split = sem("rw_split")
        x_in = sem("x_in")
        xr_in = sem("xr_in")
        ctx_in = sem("ctx_in")
        q_low_ready = sem("q_low_ready")
        q_high_ready = sem("q_high_ready")
        acc_free = sem("acc_free")
        set_pool = sem("set_pool")
        three_ready = sem("three_ready")
        set_dve = sem("set_dve")
        tg_ready = sem("tg_ready")
        bias_mm = sem("bias_mm")
        bias_ready = sem("bias_ready")
        ln_step = [sem("ln1_step"), sem("ln2_step")]
        half_done = [sem("half1_done"), sem("half2_done")]
        seeded = [sem("seeded1"), sem("seeded2")]
        newton = [sem("newton1"), sem("newton2")]
        xn_first, xT_first_mm, xT_first = sem("xn_first"), sem("xT_first_mm"), sem("xT_first")
        q_first_mm, q_first = sem("q_first_mm"), sem("q_first")
        xn_ready = sem("xn_ready")
        xT_mm = sem("xT_mm")
        xT_ready = sem("xT_ready")
        kv_mm = sem("kv_mm")
        k_ready = sem("k_ready")
        v_ready = sem("v_ready")
        q_mm = sem("q_mm")
        q_ready = sem("q_ready")
        xres_ready = sem("xres_ready")
        s_mm = sem("s_mm")
        part_ready = sem("part_ready")
        other_ready = sem("other_ready")
        m_ready = sem("m_ready")
        mexp_ready = sem("mexp_ready")
        shift_mm = sem("shift_mm")
        p_ready = sem("p_ready")
        av_mm = sem("av_mm")
        rden_ready = sem("rden_ready")
        u_ready = sem("u_ready")
        wo_mm = sem("wo_mm")
        x2_ready = sem("x2_ready")
        x2n_ready = sem("x2n_ready")
        x2T_mm = sem("x2T_mm")
        x2h_ready = sem("x2h_ready")
        x2l_ready = sem("x2l_ready")
        rt_mm = sem("rt_mm")
        low_done = sem("low_done")
        lg_ready = sem("lg_ready")
        ldiff_ready = sem("ldiff_ready")
        lexp_ready = sem("lexp_ready")
        gate_step = sem("gate_step")
        a1_mm = sem("a1_mm")
        a3_mm = sem("a3_mm")
        th_ready = sem("th_ready")
        sl_ready = sem("sl_ready")
        h_ready = sem("h_ready")
        y_mm = sem("y_mm")
        y_scaled = sem("y_scaled")
        ys_free = sem("ys_free")
        x2_kept_ready = sem("x2_kept_ready")

        LN_STEPS = PAIRS + 8
        NEWTON_STEPS = (4 * NEWTON, 3 * NEWTON)
        GATE_STEPS = 12

        def wait(eng, s, value):
            if not isinstance(value, int) or value > 0:
                eng.wait_ge(s, value)

        block = ctx.enter_context(nc.Block())

        @block.sync
        def _(sp):
            def load_ctx(n):
                wait(sp, kv_mm, 2 * n)
                sp.dma_start(ctxT[:], ctx_t[:, bass.ts(n, CHUNK)]).then_inc(ctx_in, 16)

            def load_x(n):
                wait(sp, xn_ready, n)
                sp.dma_start(xc[:], x[bass.ts(n, CHUNK), :].rearrange("(t p) d -> p t d", p=D))\
                    .then_inc(x_in, 16)

            def load_residual(n):
                wait(sp, xres_ready, n)
                sp.dma_start(xr[:], x[bass.ts(n, CHUNK), :].rearrange("(t p) d -> p t d", p=D))\
                    .then_inc(xr_in, 16)

            def store(n):
                sp.wait_ge(ys_free, 2 + ALL_E * (n + 1))
                sp.dma_start(out[bass.ts(n, CHUNK), :].rearrange("(t p) d -> p t d", p=D), acc[:])\
                    .then_inc(acc_free, 16)

            sp.sem_inc(acc_free, 16)
            load_x(0)
            sp.dma_start(proj_in[:], proj_w).then_inc(proj_loaded, 16)
            load_ctx(0)
            sp.dma_start(rest_in[:], rest_w).then_inc(rest_loaded, 16)
            sp.dma_start(rows_in[:], rows.rearrange("(a n) -> a n", a=1).to_broadcast([D, rows.shape[0]]))\
                .then_inc(rest_loaded, 16)
            sp.dma_start(W1[:].rearrange("p e n -> p (e n)"), w1).then_inc(up_in, 16)
            sp.dma_start(W3[:].rearrange("p e n -> p (e n)"), w3).then_inc(up_in, 16)
            sp.dma_start(W2[:].rearrange("p e n -> p (e n)"), w2).then_inc(down_in, 16)
            load_residual(0)
            load_x(1)
            load_ctx(1)
            load_residual(1)

            def body(n):
                load_ctx(n + 2)
                load_x(n + 2)
                load_residual(n + 2)
                store(n)

            with sp.Fori(0, NCH - 2) as n:
                body(n)
            store(NCH - 2)
            store(NCH - 1)
            sp.wait_ge(acc_free, 16 * (NCH + 1))

        @block.gpsimd
        def _(pool):
            def spread_max(n, u):
                pool.wait_ge(m_ready, UNITS * n + u + 1)
                wait(pool, shift_mm, UNITS * n + u - 1)
                pool.tensor_tensor(
                    m_exp[:, u % 2, :].rearrange("p (k c) -> p k c", c=QUAD),
                    eye.unsqueeze(1).to_broadcast([D, 16, QUAD]),
                    m_all[:, :].unsqueeze(2).to_broadcast([D, 16, QUAD]), ALU.mult)\
                    .then_inc(mexp_ready, 1)

            def rsqrt_steps(n):
                y, v, t, s = rstd[0], neg_half[0], nwt[0], newton[0]
                pool.wait_ge(seeded[0], n + 1)
                at = NEWTON_STEPS[0] * n
                for step in range(NEWTON):
                    wait(pool, s, at)
                    pool.tensor_tensor(t[:], y[:], y[:], ALU.mult).then_inc(s, 1)
                    pool.wait_ge(s, at + 1)
                    pool.tensor_tensor(t[:], t[:], v[:], ALU.mult).then_inc(s, 1)
                    pool.wait_ge(s, at + 2)
                    pool.tensor_tensor(t[:], t[:], three_halves[:], ALU.add).then_inc(s, 1)
                    pool.wait_ge(s, at + 3)
                    pool.tensor_tensor(y[:], y[:], t[:], ALU.mult).then_inc(s, 1)
                    at = at + 4

            def residual_in(n):
                pool.wait_ge(xr_in, 16 * (n + 1))
                wait(pool, x2_ready, PAIRS * n)
                if is_first(n):
                    pool.wait_ge(bias_ready, 2)
                pool.tensor_tensor(xres[:], xr[:], bias_row[:, :].unsqueeze(1).to_broadcast([D, PAIRS, D]),
                                   ALU.add).then_inc(xres_ready, 1)

            def add(n, e):
                at = ALL_E * n + e
                pool.wait_ge(y_scaled, at + 1)
                if e == 0:
                    pool.wait_ge(acc_free, 16 * (n + 1))
                    pool.wait_ge(x2_kept_ready, n + 1)
                else:
                    pool.wait_ge(ys_free, 2 + at)
                pool.tensor_tensor(acc[:], ys[:, e % 2], (acc if e else x2_kept)[:], ALU.add).then_inc(ys_free, 1)

            def middle(n, m, c):
                spread_max(n, 3)
                spread_max(n, 4)
                if c is not None:
                    rsqrt_steps(c)
                spread_max(n, 5)
                add(m, 0)
                add(m, 1)
                spread_max(n, 6)
                add(m, 2)

            def ends(n, m, c):
                spread_max(n, 7)
                add(m, 3)
                if c is not None:
                    spread_max(c, 0)
                add(m, 4)
                add(m, 5)
                if c is not None:
                    spread_max(c, 1)
                add(m, 6)
                add(m, 7)
                if c is not None:
                    spread_max(c, 2)
                add(m, 8)
                if c is not None:
                    residual_in(c)

            def split(part, hi, src):
                pool.wait_ge(split_hi, 2)
                pool.tensor_tensor(part[:], src[:], hi[:].bitcast(F32), ALU.subtract).then_inc(split_lo, 1)

            pool.sem_inc(ys_free, 2)
            pool.memset(three_halves[:], 1.5).then_inc(three_ready, 1)
            pool.memset(v_w[:], 0.0).then_inc(set_pool, 1)
            pool.wait_ge(three_ready, 1)
            residual_in(0)
            spread_max(0, 0)
            spread_max(0, 1)
            spread_max(0, 2)
            spread_max(0, 3)
            spread_max(0, 4)
            rsqrt_steps(1)
            spread_max(0, 5)
            spread_max(0, 6)
            spread_max(0, 7)
            spread_max(1, 0)
            residual_in(1)
            spread_max(1, 1)
            split(W1l, W1h, W1)
            split(W3l, W3h, W3)
            spread_max(1, 2)
            with pool.Fori(0, NCH - 2) as m:
                middle(m + 1, m, m + 2)
                ends(m + 1, m, m + 2)
            middle(NCH - 1, NCH - 2, None)
            ends(NCH - 1, NCH - 2, None)
            add(NCH - 1, 0)
            add(NCH - 1, 1)
            add(NCH - 1, 2)
            add(NCH - 1, 3)
            add(NCH - 1, 4)
            add(NCH - 1, 5)
            add(NCH - 1, 6)
            add(NCH - 1, 7)

        @block.scalar
        def _(act):
            def keys_out(n, hf, bank=M0):
                act.wait_ge(kv_mm, 2 * n + hf + 1)
                act.activation(kT[:, hf * HALF:(hf + 1) * HALF], bank[:, 0:HALF], ACT.Identity, bias=col[:, 1:2])\
                    .then_inc(k_ready, 1)

            def values_out(n, hf, bank=M0):
                act.wait_ge(kv_mm, 2 * n + hf + 1)
                src = bank[:, HALF:].rearrange("p (k a d) -> p k a d", a=2, d=HD)
                flat = v_w[:, hf * 2:hf * 2 + 2].rearrange("p t (k a) c -> p (t k) (a c)", a=2)
                for b in range(2):
                    for a in range(2):
                        at = a * (QUAD + 2 * HD) + b * HD
                        last = act.activation(flat[:, :, at:at + HD], src[:, :, a, :], ACT.Copy,
                                              scale=cst[:, C_MASK + b:C_MASK + b + 1])
                last.then_inc(v_ready, 1)

            def xT_out(n):
                act.wait_ge(xT_mm, n + 1)
                act.activation(xnT[:], M0[:], ACT.Copy).then_inc(xT_ready, 1)

            def queries_out(n):
                act.wait_ge(q_mm, n + 1)
                wait(act, q_low_ready, 2 * n)
                wait(act, q_high_ready, 2 * n)
                act.activation(qT[:], M0[:], ACT.Identity, bias=col[:, 0:1]).then_inc(q_ready, 1)

            def spread_q(n, hf, first, count):
                if is_first(n) and hf == 0:
                    act.wait_ge(q_first, 1)
                else:
                    act.wait_ge(q_ready, n + 1)
                if hf:
                    wait(act, s_mm, UNITS * n)
                tok = slice(hf * HALF, (hf + 1) * HALF)
                for hd in range(first, first + count):
                    last = act.activation(q_blk[:, hd, tok], qT[:, tok], ACT.Copy,
                                          scale=cst[:, C_HEAD + hd:C_HEAD + hd + 1])
                if first + count == UH:
                    last.then_inc(q_low_ready, 1)
                if first + count == HEADS:
                    last.then_inc(q_high_ready, 1)

            def probs(n, u):
                act.wait_ge(shift_mm, UNITS * n + u + 1)
                if u % 2 == 0:
                    wait(act, av_mm, PAIRS * n + u // 2 - 1)
                half_heads = P[:, (u // 2) % 2, (u % 2) * UH:(u % 2 + 1) * UH, :]
                act.activation(half_heads.rearrange("p a b -> p (a b)"), score_bank(n, u)[:], ACT.Exp, scale=SCALE)\
                    .then_inc(p_ready, 1)

            def tanh_half(n, e):
                k = two_banks(n, e)
                act.wait_ge(a1_mm, ALL_E * n + e + 1)
                act.activation(th[:, k, :], A1s[k][:], ACT.Tanh, scale=0.5).then_inc(th_ready, 1)

            def weigh(n, e):
                k = two_banks(n, e)
                at = ALL_E * n + e
                if e == 0:
                    act.wait_ge(gate_step, GATE_STEPS * (n + 1))
                act.wait_ge(y_mm, at + 1)
                act.wait_ge(ys_free, at + (1 if e else 2))
                for t in range(PAIRS):
                    weight = gate[:, t, e:e + 1] if e < EXPERTS else tg[:, 1:2]
                    last = act.activation(ys[:, e % 2, t, :], Ys[k][:, t * D:(t + 1) * D], ACT.Copy, scale=weight)
                last.then_inc(y_scaled, 1)

            def x2T_out(n):
                act.wait_ge(x2T_mm, n + 1)
                act.activation(x2h[:], M1[:], ACT.Copy).then_inc(x2h_ready, 1)

            def keep_x2(n):
                act.wait_ge(x2_ready, PAIRS * (n + 1))
                act.activation(x2_kept[:], x2[:], ACT.Copy).then_inc(x2_kept_ready, 1)

            def router_exp(n):
                act.wait_ge(ldiff_ready, n + 1)
                act.activation(lexp[:], lg[:], ACT.Exp).then_inc(lexp_ready, 1)

            def middle(n, m, c):
                x2T_out(m)
                keep_x2(m)
                tanh_half(m, 0)
                probs(n, 2)
                router_exp(m)
                probs(n, 3)
                tanh_half(m, 1)
                tanh_half(m, 2)
                weigh(m, 0)
                probs(n, 4)
                weigh(m, 1)
                tanh_half(m, 3)
                if c is not None:
                    xT_out(c)
                probs(n, 5)
                if c is not None:
                    queries_out(c)
                    spread_q(c, 0, 8, 2)
                weigh(m, 2)
                if c is not None:
                    spread_q(c, 0, 10, 2)
                    spread_q(c, 0, 12, 2)
                    spread_q(c, 0, 14, 2)
                tanh_half(m, 4)
                weigh(m, 3)
                probs(n, 6)
                if c is not None:
                    keys_out(c, 0)
                    spread_q(c, 1, 0, 2)

            def ends(n, m, c):
                if c is not None:
                    spread_q(c, 1, 2, 2)
                tanh_half(m, 5)
                probs(n, 7)
                if c is not None:
                    spread_q(c, 1, 4, 2)
                weigh(m, 4)
                if c is not None:
                    spread_q(c, 1, 6, 2)
                tanh_half(m, 6)
                if c is not None:
                    spread_q(c, 1, 8, 2)
                    values_out(c, 0)
                    spread_q(c, 1, 10, 2)
                weigh(m, 5)
                tanh_half(m, 7)
                if c is not None:
                    spread_q(c, 1, 12, 2)
                    keys_out(c, 1)
                    probs(c, 0)
                weigh(m, 6)
                tanh_half(m, 8)
                if c is not None:
                    values_out(c, 1)
                    probs(c, 1)
                weigh(m, 7)
                if c is not None:
                    spread_q(c, 1, 14, 2)
                weigh(m, 8)

            def split(part, src):
                act.wait_ge(up_in, 32)
                act.activation(part[:], src[:], ACT.Copy).then_inc(split_hi, 1)

            act.wait_ge(proj_loaded, 16)
            keys_out(0, 0, A1)
            act.wait_ge(xT_first_mm, 1)
            act.activation(xnT[:, 0:HALF], M0[:, 0:HALF], ACT.Copy).then_inc(xT_first, 1)
            act.wait_ge(rest_loaded, 32)
            act.activation(tg[:], gate_in, ACT.Tanh).then_inc(tg_ready, 1)
            act.wait_ge(q_first_mm, 1)
            act.activation(qT[:, 0:HALF], Y[:, 0:HALF], ACT.Identity, bias=col[:, 0:1]).then_inc(q_first, 1)
            act.wait_ge(xT_mm, 1)
            act.activation(xnT[:, HALF:], M0[:, HALF:], ACT.Copy).then_inc(xT_ready, 1)
            spread_q(0, 0, UH, 4)
            act.wait_ge(q_mm, 1)
            act.activation(qT[:, HALF:], Y[:, HALF:], ACT.Identity, bias=col[:, 0:1]).then_inc(q_ready, 1)
            spread_q(0, 0, UH + 4, 4)
            act.wait_ge(set_pool, 1)
            act.wait_ge(tg_ready, 1)
            values_out(0, 0, A1)
            spread_q(0, 1, 8, 2)
            keys_out(0, 1, A3)
            spread_q(0, 1, 10, 2)
            probs(0, 0)
            spread_q(0, 1, 12, 2)
            spread_q(0, 1, 14, 2)
            probs(0, 1)
            values_out(0, 1, A3)
            probs(0, 2)
            probs(0, 3)
            xT_out(1)
            probs(0, 4)
            probs(0, 5)
            queries_out(1)
            spread_q(1, 0, 8, 2)
            probs(0, 6)
            keys_out(1, 0)
            spread_q(1, 0, 10, 2)
            spread_q(1, 0, 12, 2)
            probs(0, 7)
            spread_q(1, 0, 14, 2)
            spread_q(1, 1, 0, 2)
            values_out(1, 0)
            split(W1h, W1)
            spread_q(1, 1, 2, 2)
            values_out(1, 1)
            spread_q(1, 1, 4, 2)
            probs(1, 0)
            split(W3h, W3)
            spread_q(1, 1, 6, 2)
            spread_q(1, 1, 8, 2)
            keys_out(1, 1)
            probs(1, 1)
            spread_q(1, 1, 10, 2)
            spread_q(1, 1, 12, 2)
            spread_q(1, 1, 14, 2)
            with act.Fori(0, NCH - 2) as m:
                middle(m + 1, m, m + 2)
                ends(m + 1, m, m + 2)
            middle(NCH - 1, NCH - 2, None)
            ends(NCH - 1, NCH - 2, None)
            x2T_out(NCH - 1)
            tanh_half(NCH - 1, 0)
            router_exp(NCH - 1)
            tanh_half(NCH - 1, 1)
            tanh_half(NCH - 1, 2)
            keep_x2(NCH - 1)
            tanh_half(NCH - 1, 3)
            weigh(NCH - 1, 0)
            weigh(NCH - 1, 1)
            tanh_half(NCH - 1, 4)
            weigh(NCH - 1, 2)
            tanh_half(NCH - 1, 5)
            weigh(NCH - 1, 3)
            tanh_half(NCH - 1, 6)
            tanh_half(NCH - 1, 7)
            weigh(NCH - 1, 4)
            weigh(NCH - 1, 5)
            tanh_half(NCH - 1, 8)
            weigh(NCH - 1, 6)
            weigh(NCH - 1, 7)

        @block.vector
        def _(dve):
            def norm_stats(n, k, src, t):
                dve.bn_stats(st[k][:, t, :], src[:, t, :]).then_inc(ln_step[k], 1)

            def norm_sums(n, k):
                s, at = ln_step[k], LN_STEPS * n + PAIRS
                even, odd = st[k][:, :, 0:3], st[k][:, :, 3:6]
                dve.wait_ge(s, at)
                dve.tensor_tensor(dm[k][:], even[:, :, 1], odd[:, :, 1], ALU.subtract).then_inc(s, 1)
                dve.tensor_tensor(sm[k][:], even[:, :, 1], odd[:, :, 1], ALU.add).then_inc(s, 1)
                dve.tensor_tensor(cv[k][:], even[:, :, 2], odd[:, :, 2], ALU.add).then_inc(s, 1)

            def norm_moments(n, k):
                s, at = ln_step[k], LN_STEPS * n + PAIRS
                dve.wait_ge(s, at + 1)
                dve.scalar_tensor_tensor(out=dm[k][:], in0=dm[k][:], scalar=0.25, in1=dm[k][:],
                                         op0=ALU.mult, op1=ALU.mult).then_inc(s, 1)
                dve.wait_ge(s, at + 2)
                dve.tensor_scalar(mean[k][:], sm[k][:], 0.5, None, ALU.mult).then_inc(s, 1)
                dve.wait_ge(s, at + 3)
                dve.tensor_scalar(cv[k][:], cv[k][:], 1.0 / D, EPS, ALU.mult, ALU.add).then_inc(s, 1)

            def norm_var(n, k):
                s, at = ln_step[k], LN_STEPS * n + PAIRS
                dve.wait_ge(s, at + 6)
                wait(dve, newton[k], NEWTON_STEPS[k] * n)
                dve.tensor_tensor(var[k][:], cv[k][:], dm[k][:], ALU.add).then_inc(s, 1)

            def norm_half(n, k):
                s, at = ln_step[k], LN_STEPS * n + PAIRS
                dve.wait_ge(s, at + 7)
                dve.tensor_scalar(neg_half[k][:], var[k][:], -0.5, None, ALU.mult).then_inc(s, 1)
                dve.tensor_scalar(half[k][:].bitcast(I32), var[k][:].bitcast(I32), 1, None,
                                  ALU.logical_shift_right).then_inc(half_done[k], 1)

            def norm_guess(n, k):
                dve.wait_ge(half_done[k], n + 1)
                dve.wait_ge(ln_step[k], LN_STEPS * (n + 1))
                dve.tensor_scalar(rstd[k][:].bitcast(I32), half[k][:].bitcast(I32), -1.0, RSQRT_SEED,
                                  ALU.mult, ALU.add).then_inc(seeded[k], 1)

            def rsqrt_step(n, step):
                y, v, t, s = rstd[1], neg_half[1], nwt[1], newton[1]
                at = NEWTON_STEPS[1] * n + 3 * step
                if step:
                    dve.wait_ge(s, at)
                else:
                    dve.wait_ge(seeded[1], n + 1)
                dve.tensor_tensor(t[:], y[:], y[:], ALU.mult).then_inc(s, 1)
                dve.wait_ge(s, at + 1)
                dve.tensor_tensor(t[:], t[:], v[:], ALU.mult).then_inc(s, 1)
                dve.wait_ge(s, at + 2)
                dve.scalar_tensor_tensor(out=y[:], in0=t[:], scalar=1.5, in1=y[:], op0=ALU.add, op1=ALU.mult)\
                    .then_inc(s, 1)

            def first_rsqrt():
                y, v, t, s = rstd[0], neg_half[0], nwt[0], newton[0]
                dve.wait_ge(seeded[0], 1)
                for at in range(0, 3 * NEWTON, 3):
                    wait(dve, s, at)
                    dve.tensor_tensor(t[:], y[:], y[:], ALU.mult).then_inc(s, 1)
                    dve.wait_ge(s, at + 1)
                    dve.tensor_tensor(t[:], t[:], v[:], ALU.mult).then_inc(s, 1)
                    dve.wait_ge(s, at + 2)
                    last = at == 3 * (NEWTON - 1)
                    dve.scalar_tensor_tensor(out=y[:], in0=t[:], scalar=1.5, in1=y[:], op0=ALU.add, op1=ALU.mult)\
                        .then_inc(s, 1 + NEWTON if last else 1)

            def norm_apply(n, k, src, dst, done, first=0, count=PAIRS):
                dve.wait_ge(newton[k], NEWTON_STEPS[k] * (n + 1))
                for t in range(first, first + count):
                    last = dve.tensor_scalar(dst[:, t, :], src[:, t, :], mean[k][:, t:t + 1], rstd[k][:, t:t + 1],
                                             ALU.subtract, ALU.mult)
                last.then_inc(done, 1)

            def x_stats(n):
                dve.wait_ge(x_in, 16 * (n + 1))
                for t in range(PAIRS):
                    norm_stats(n, 0, xc, t)

            def x_norm(n):
                wait(dve, xT_mm, n)
                norm_apply(n, 0, xc, xn, xn_ready)

            def x2_norm(n):
                wait(dve, x2T_mm, n)
                norm_apply(n, 1, x2, x2n, x2n_ready)

            def spread_q(n, hf, first, count):
                if is_first(n) and hf == 0:
                    dve.wait_ge(q_first, 1)
                else:
                    dve.wait_ge(q_ready, n + 1)
                if hf:
                    wait(dve, s_mm, UNITS * n)
                tok = slice(hf * HALF, (hf + 1) * HALF)
                for hd in range(first, first + count):
                    last = dve.tensor_scalar(q_blk[:, hd, tok], qT[:, tok], cst[:, C_HEAD + hd:C_HEAD + hd + 1],
                                             None, ALU.mult)
                if first + count == UH:
                    last.then_inc(q_low_ready, 1)

            def quad_max(n, u):
                at = UNITS * n + u
                dve.wait_ge(s_mm, at + 1)
                wait(dve, m_ready, at)
                dve.tensor_reduce(m_part[:], score_bank(n, u)[:].rearrange("p (k c) -> p k c", c=QUAD), AX_X,
                                  ALU.max, apply_transpose=True).then_inc(part_ready, 1)

            def other_quad(n, u):
                dve.wait_ge(part_ready, UNITS * n + u + 1)
                for b in range(2):
                    last = dve.tensor_copy(m_other[b * SEQ:b * SEQ + QUAD, :],
                                           m_part[b * SEQ + QUAD:(b + 1) * SEQ, :])
                last.then_inc(other_ready, 1)

            def batch_max(n, u):
                at = UNITS * n + u
                dve.wait_ge(other_ready, at + 1)
                wait(dve, mexp_ready, at)
                dve.tensor_tensor(m_all[:], m_part[:], m_other[:], ALU.max).then_inc(m_ready, 1)

            def inverse(n, t):
                at = PAIRS * n + t
                dve.wait_ge(av_mm, at + 1)
                wait(dve, u_ready, at)
                dve.reciprocal(rden[:], AV[:, D:2 * D]).then_inc(rden_ready, 1)

            def normalise(n, t):
                at = PAIRS * n + t
                dve.wait_ge(rden_ready, at + 1)
                wait(dve, wo_mm, at)
                dve.tensor_tensor(U[:], AV[:, 0:D], rden[:], ALU.mult).then_inc(u_ready, 1)

            def residual(n, t):
                at = PAIRS * n + t
                dve.wait_ge(wo_mm, at + 1)
                if t == 0:
                    dve.wait_ge(xres_ready, n + 1)
                    wait(dve, x2_kept_ready, n)
                dve.scalar_tensor_tensor(out=x2[:, t, :], in0=M1[:, t * D:(t + 1) * D], scalar=tg[:, 0:1],
                                         in1=xres[:, t, :], op0=ALU.mult, op1=ALU.add).then_inc(x2_ready, 1)
                dve.wait_ge(x2_ready, at + 1)
                norm_stats(n, 1, x2, t)

            def logits(n):
                dve.wait_ge(rt_mm, n + 1)
                parts = M1[:, 0:2 * PAIRS * EXPERTS].rearrange("p (t k e) -> p t k e", k=2, e=EXPERTS)
                dve.tensor_copy(lg[:], parts[:, :, 0, :]).then_inc(low_done, 1)
                dve.wait_ge(low_done, n + 1)
                dve.tensor_tensor(lg[:], lg[:], parts[:, :, 1, :], ALU.add).then_inc(lg_ready, 1)

            def logit_max(n):
                dve.wait_ge(lg_ready, n + 1)
                dve.tensor_reduce(lmax[:], lg[:], AX_X, ALU.max).then_inc(gate_step, 1)

            def logit_diff(n):
                dve.wait_ge(gate_step, GATE_STEPS * n + 1)
                dve.tensor_tensor(lg[:], lg[:], over(lmax), ALU.subtract).then_inc(ldiff_ready, 1)

            def exp_sum(n):
                dve.wait_ge(lexp_ready, n + 1)
                dve.tensor_reduce(lsum[:], lexp[:], AX_X, ALU.add).then_inc(gate_step, 1)

            def exp_inverse(n):
                dve.wait_ge(gate_step, GATE_STEPS * n + 2)
                dve.reciprocal(lsum[:], lsum[:]).then_inc(gate_step, 1)

            def expert_score(n):
                dve.wait_ge(gate_step, GATE_STEPS * n + 3)
                dve.tensor_tensor(score[:], lexp[:], over(lsum), ALU.mult).then_inc(gate_step, 1)

            def expert_bias(n):
                dve.wait_ge(gate_step, GATE_STEPS * n + 4)
                dve.tensor_tensor(biased[:], score[:], eb.unsqueeze(1).to_broadcast([D, PAIRS, EXPERTS]),
                                  ALU.add).then_inc(gate_step, 1)
                dve.tensor_scalar(score[:], score[:], tg[:, 1:2], None, ALU.mult).then_inc(gate_step, 1)

            def compare(n):
                other = biased[:].unsqueeze(2).to_broadcast([D, PAIRS, EXPERTS, EXPERTS])
                dve.wait_ge(gate_step, GATE_STEPS * n + 5)
                dve.tensor_tensor(level[:], other, by_expert(biased), ALU.is_ge).then_inc(gate_step, 1)
                dve.tensor_tensor(above[:], other, by_expert(biased), ALU.is_gt).then_inc(gate_step, 1)

            def same_and_lower(n):
                dve.wait_ge(gate_step, GATE_STEPS * n + 7)
                dve.tensor_tensor(level[:].rearrange("p t e f -> p t (e f)"),
                                  level[:].rearrange("p t e f -> p t (e f)"),
                                  low.unsqueeze(1).to_broadcast([D, PAIRS, EXPERTS * EXPERTS]), ALU.mult)\
                    .then_inc(gate_step, 1)

            def ahead(n):
                pairwise = above[:].rearrange("p t e f -> p (t e) f")
                dve.wait_ge(gate_step, GATE_STEPS * n + 9)
                dve.tensor_tensor(pairwise, pairwise, level[:].rearrange("p t e f -> p (t e) f"), ALU.max)\
                    .then_inc(gate_step, 1)

            def expert_rank(n):
                dve.wait_ge(gate_step, GATE_STEPS * n + 10)
                dve.tensor_reduce(rank[:].rearrange("p t e -> p (t e)"), above[:].rearrange("p t e f -> p (t e) f"),
                                  AX_X, ALU.add).then_inc(gate_step, 1)

            def top_two(n):
                dve.wait_ge(gate_step, GATE_STEPS * n + 11)
                dve.scalar_tensor_tensor(out=gate[:], in0=rank[:], scalar=1.5, in1=score[:],
                                         op0=ALU.is_lt, op1=ALU.mult).then_inc(gate_step, 1)

            def over(a):
                return a[:, :].unsqueeze(2).to_broadcast([D, PAIRS, EXPERTS])

            def by_expert(a):
                return a[:].unsqueeze(3).to_broadcast([D, PAIRS, EXPERTS, EXPERTS])

            def x2_low(n):
                dve.wait_ge(x2h_ready, n + 1)
                dve.tensor_tensor(x2l[:], M1[:], x2h[:].bitcast(F32), ALU.subtract).then_inc(x2l_ready, 1)

            def silu(n, e):
                k = two_banks(n, e)
                at = ALL_E * n + e
                dve.wait_ge(th_ready, at + 1)
                if e:
                    dve.wait_ge(h_ready, at)
                dve.scalar_tensor_tensor(out=sl[:], in0=th[:, k, :], scalar=1.0, in1=A1s[k][:],
                                         op0=ALU.add, op1=ALU.mult)\
                    .then_inc(sl_ready, 1)

            def finish(n, e):
                dve.wait_ge(y_mm, ALL_E * n + e + 1)
                dve.wait_ge(ys_free, 2 + ALL_E * n + e)
                for t in range(PAIRS):
                    last = dve.scalar_tensor_tensor(out=acc[:, t, :], in0=Ys[two_banks(n, e)][:, t * D:(t + 1) * D],
                                                    scalar=tg[:, 1:2], in1=acc[:, t, :], op0=ALU.mult, op1=ALU.add)
                last.then_inc(ys_free, 1)

            def hidden(n, e):
                k = two_banks(n, e)
                at = ALL_E * n + e
                dve.wait_ge(a3_mm, at + 1)
                dve.wait_ge(sl_ready, at + 1)
                if e > 1:
                    dve.wait_ge(y_mm, at - 1)
                dve.scalar_tensor_tensor(out=h[:, e % 2, :], in0=A3s[k][:], scalar=0.5, in1=sl[:],
                                         op0=ALU.mult, op1=ALU.mult).then_inc(h_ready, 1)

            def middle(n, m, c):
                x2_low(m)
                quad_max(n, 3)
                other_quad(n, 3)
                silu(m, 0)
                logits(m)
                batch_max(n, 3)
                logit_max(m)
                hidden(m, 0)
                logit_diff(m)
                residual(n, 0)
                exp_sum(m)
                quad_max(n, 4)
                if c is not None:
                    x_stats(c)
                exp_inverse(m)
                if c is not None:
                    norm_sums(c, 0)
                expert_score(m)
                other_quad(n, 4)
                expert_bias(m)
                compare(m)
                batch_max(n, 4)
                same_and_lower(m)
                silu(m, 1)
                ahead(m)
                if c is not None:
                    norm_moments(c, 0)
                    norm_var(c, 0)
                expert_rank(m)
                if c is not None:
                    norm_half(c, 0)
                top_two(m)
                if c is not None:
                    norm_guess(c, 0)
                hidden(m, 1)
                silu(m, 2)
                quad_max(n, 5)
                inverse(n, 1)
                other_quad(n, 5)
                batch_max(n, 5)
                normalise(n, 1)
                if c is not None:
                    x_norm(c)
                hidden(m, 2)
                quad_max(n, 6)
                silu(m, 3)
                other_quad(n, 6)
                batch_max(n, 6)
                residual(n, 1)
                hidden(m, 3)
                if c is not None:
                    spread_q(c, 0, 0, 2)
                inverse(n, 2)
                if c is not None:
                    spread_q(c, 0, 2, 2)
                quad_max(n, 7)
                normalise(n, 2)
                if c is not None:
                    spread_q(c, 0, 4, 2)
                other_quad(n, 7)
                batch_max(n, 7)
                if c is not None:
                    spread_q(c, 0, 6, 2)

            def ends(n, m, c):
                silu(m, 4)
                hidden(m, 4)
                silu(m, 5)
                residual(n, 2)
                hidden(m, 5)
                inverse(n, 3)
                if c is not None:
                    quad_max(c, 0)
                    other_quad(c, 0)
                normalise(n, 3)
                silu(m, 6)
                if c is not None:
                    batch_max(c, 0)
                    quad_max(c, 1)
                hidden(m, 6)
                if c is not None:
                    other_quad(c, 1)
                residual(n, 3)
                if c is not None:
                    batch_max(c, 1)
                norm_sums(n, 1)
                silu(m, 7)
                norm_moments(n, 1)
                norm_var(n, 1)
                hidden(m, 7)
                norm_half(n, 1)
                norm_guess(n, 1)
                rsqrt_step(n, 0)
                if c is not None:
                    quad_max(c, 2)
                silu(m, 8)
                rsqrt_step(n, 1)
                hidden(m, 8)
                if c is not None:
                    other_quad(c, 2)
                    batch_max(c, 2)
                rsqrt_step(n, 2)
                x2_norm(n)
                if c is not None:
                    inverse(c, 0)
                    normalise(c, 0)

            dve.memset(m_other[:], 0.0).then_inc(set_dve, 1)
            dve.memset(bv_rep[:], 0.0).then_inc(set_dve, 1)
            x_stats(0)
            for step in (norm_sums, norm_moments, norm_var, norm_half, norm_guess):
                step(0, 0)
            first_rsqrt()
            dve.wait_ge(proj_loaded, 16)
            dve.wait_ge(set_dve, 2)
            dve.tensor_scalar(bv_rep[:], bv_rep[:], col[:, 2:3], None, ALU.add).then_inc(set_dve, 1)
            norm_apply(0, 0, xc, xn, xn_first, 0, 2)
            norm_apply(0, 0, xc, xn, xn_ready, 2, 2)
            dve.wait_ge(rest_loaded, 32)
            dve.tensor_copy(negr[:], cst[:, C_NEG:C_NEG + D]).then_inc(set_dve, 1)
            dve.tensor_copy(rwh, rw).then_inc(set_dve, 1)
            dve.wait_ge(set_dve, 5)
            dve.tensor_tensor(rwl, rw, rwh.bitcast(F32), ALU.subtract).then_inc(rw_split, 1)
            dve.wait_ge(bias_mm, 1)
            dve.tensor_tensor(bias_sum[:], M1[:, 0:D], bo_row, ALU.add).then_inc(bias_ready, 1)
            dve.wait_ge(bias_ready, 1)
            dve.wait_ge(tg_ready, 1)
            dve.tensor_scalar(bias_row[:], bias_sum[:], tg[:, 0:1], None, ALU.mult).then_inc(bias_ready, 1)
            spread_q(0, 0, 0, UH)
            x_stats(1)
            spread_q(0, 1, 0, 2)
            quad_max(0, 0)
            other_quad(0, 0)
            batch_max(0, 0)
            quad_max(0, 1)
            other_quad(0, 1)
            batch_max(0, 1)
            spread_q(0, 1, 2, 2)
            spread_q(0, 1, 4, 2)
            quad_max(0, 2)
            other_quad(0, 2)
            norm_sums(1, 0)
            batch_max(0, 2)
            norm_moments(1, 0)
            spread_q(0, 1, 6, 2)
            norm_var(1, 0)
            quad_max(0, 3)
            norm_half(1, 0)
            other_quad(0, 3)
            batch_max(0, 3)
            quad_max(0, 4)
            other_quad(0, 4)
            norm_guess(1, 0)
            batch_max(0, 4)
            inverse(0, 0)
            normalise(0, 0)
            quad_max(0, 5)
            other_quad(0, 5)
            batch_max(0, 5)
            residual(0, 0)
            inverse(0, 1)
            x_norm(1)
            normalise(0, 1)
            quad_max(0, 6)
            other_quad(0, 6)
            batch_max(0, 6)
            quad_max(0, 7)
            other_quad(0, 7)
            spread_q(1, 0, 0, 2)
            spread_q(1, 0, 2, 2)
            spread_q(1, 0, 4, 2)
            batch_max(0, 7)
            residual(0, 1)
            spread_q(1, 0, 6, 2)
            inverse(0, 2)
            normalise(0, 2)
            quad_max(1, 0)
            residual(0, 2)
            other_quad(1, 0)
            batch_max(1, 0)
            inverse(0, 3)
            normalise(0, 3)
            quad_max(1, 1)
            other_quad(1, 1)
            residual(0, 3)
            batch_max(1, 1)
            norm_sums(0, 1)
            norm_moments(0, 1)
            quad_max(1, 2)
            norm_var(0, 1)
            norm_half(0, 1)
            norm_guess(0, 1)
            rsqrt_step(0, 0)
            rsqrt_step(0, 1)
            other_quad(1, 2)
            rsqrt_step(0, 2)
            x2_norm(0)
            inverse(1, 0)
            normalise(1, 0)
            batch_max(1, 2)
            with dve.Fori(0, NCH - 2) as m:
                middle(m + 1, m, m + 2)
                ends(m + 1, m, m + 2)
            middle(NCH - 1, NCH - 2, None)
            ends(NCH - 1, NCH - 2, None)
            x2_low(NCH - 1)
            silu(NCH - 1, 0)
            logits(NCH - 1)
            logit_max(NCH - 1)
            hidden(NCH - 1, 0)
            logit_diff(NCH - 1)
            exp_sum(NCH - 1)
            exp_inverse(NCH - 1)
            expert_score(NCH - 1)
            silu(NCH - 1, 1)
            expert_bias(NCH - 1)
            compare(NCH - 1)
            same_and_lower(NCH - 1)
            hidden(NCH - 1, 1)
            ahead(NCH - 1)
            silu(NCH - 1, 2)
            expert_rank(NCH - 1)
            top_two(NCH - 1)
            hidden(NCH - 1, 2)
            silu(NCH - 1, 3)
            hidden(NCH - 1, 3)
            silu(NCH - 1, 4)
            hidden(NCH - 1, 4)
            silu(NCH - 1, 5)
            hidden(NCH - 1, 5)
            silu(NCH - 1, 6)
            hidden(NCH - 1, 6)
            silu(NCH - 1, 7)
            hidden(NCH - 1, 7)
            silu(NCH - 1, 8)
            hidden(NCH - 1, 8)
            finish(NCH - 1, 8)

        @block.tensor
        def _(pe):
            def keys_values(n, hf, bank=M0):
                pe.wait_ge(ctx_in, 16 * (n + 1))
                if bank is M0:
                    pe.wait_ge(q_ready, n + 1)
                    if hf:
                        pe.wait_ge(k_ready, 2 * n + 1)
                        pe.wait_ge(v_ready, 2 * n + 1)
                pe.matmul(bank[:, 0:HALF], wk, ctxT[:, hf * HALF:(hf + 1) * HALF], start=True, stop=True)
                for t in range(PAIRS // 2):
                    at = hf * HALF + t * D
                    last = pe.matmul(bank[:, HALF + t * D:HALF + (t + 1) * D], ctxT[:, at:at + D], wv,
                                     start=True, stop=True)
                last.then_inc(kv_mm, 1)

            def turn_x(n):
                wait(pe, v_ready, 2 * n)
                pe.wait_ge(xn_ready, n + 1)
                for t in range(PAIRS):
                    last = pe.transpose(M0[:, t * D:(t + 1) * D], xn[:, t, :], ident)
                last.then_inc(xT_mm, 1)

            def queries(n):
                pe.wait_ge(xT_ready, n + 1)
                pe.matmul(M0[:], wq, xnT[:], start=True, stop=True).then_inc(q_mm, 1)

            def scores(n, u):
                if u % 4 == 0:
                    pe.wait_ge(k_ready, 2 * n + u // 4 + 1)
                    pe.wait_ge(q_low_ready, 2 * n + u // 4 + 1)
                if u % 4 == 1:
                    pe.wait_ge(q_high_ready, 2 * n + u // 4 + 1)
                wait(pe, p_ready, u - 3 if is_first(n) else UNITS * n + u - 1)
                t, hs = u // 2, (u % 2) * UH
                for b in range(2):
                    tok = slice(t * D + b * SEQ, t * D + (b + 1) * SEQ)
                    last = pe.matmul(score_bank(n, u)[b * SEQ:(b + 1) * SEQ, :], kT[:, tok], q_blk[:, hs:hs + UH, tok],
                                     start=True, stop=False, skip_group_check=True)
                last.then_inc(s_mm, 1)

            def shift(n, u):
                pe.wait_ge(mexp_ready, UNITS * n + u + 1)
                pe.matmul(score_bank(n, u)[:], negr[:], m_exp[:, u % 2, :], start=False, stop=True,
                          skip_group_check=True).then_inc(shift_mm, 1)

            def attention(n, t):
                pe.wait_ge(p_ready, UNITS * n + 2 * t + 2)
                if t % 2 == 0:
                    pe.wait_ge(v_ready, 2 * n + t // 2 + 1)
                wait(pe, u_ready, PAIRS * n + t)
                for r in range(2):
                    for a in range(2):
                        for j in range(COLT):
                            hd = 4 * j + 2 * r + a
                            pe.matmul(AV[j * QUAD:(j + 1) * QUAD, r * SEQ:(r + 1) * SEQ], v_w[:, t, hd, :],
                                      P[:, t % 2, hd, :], start=(a == 0), stop=(a == 1), skip_group_check=True)
                for a in range(2):
                    for j in range(COLT):
                        den = cst[:, C_DEN + a * QUAD:C_DEN + (a + 1) * QUAD]
                        last = pe.matmul(AV[j * QUAD:(j + 1) * QUAD, D:2 * D], den,
                                         P[:, t % 2, 4 * j + a:4 * j + a + 3:2, :], start=(a == 0), stop=(a == 1),
                                         skip_group_check=True)
                last.then_inc(av_mm, 1)

            def project_out(n, t):
                at = PAIRS * n + t
                pe.wait_ge(u_ready, at + 1)
                if t == 0:
                    wait(pe, lg_ready, n)
                else:
                    pe.wait_ge(x2_ready, at)
                for r in range(2):
                    for b in range(2):
                        last = pe.matmul(M1[b * SEQ:(b + 1) * SEQ, t * D:(t + 1) * D], U[:, r * SEQ:(r + 1) * SEQ],
                                         wob[:, r, b, :], start=(r == 0), stop=(r == 1), skip_group_check=True)
                last.then_inc(wo_mm, 1)

            def turn_x2(n):
                pe.wait_ge(x2n_ready, n + 1)
                for t in range(PAIRS):
                    last = pe.transpose(M1[:, t * D:(t + 1) * D], x2n[:, t, :], ident)
                last.then_inc(x2T_mm, 1)

            def route(n):
                pe.wait_ge(x2l_ready, n + 1)
                for t in range(PAIRS):
                    tok, at = slice(t * D, (t + 1) * D), 2 * EXPERTS * t
                    pe.matmul(M1[:, at:at + 2 * EXPERTS], x2h[:, tok], rwhl[:], start=True, stop=False,
                              skip_group_check=True)
                    last = pe.matmul(M1[:, at:at + EXPERTS], x2l[:, tok], rwh, start=False, stop=True,
                                     skip_group_check=True)
                last.then_inc(rt_mm, 1)

            def product(dst, hi, lo, xh, xl):
                pe.matmul(dst, hi, xh, start=True, stop=False)
                pe.matmul(dst, lo, xh, start=False, stop=False)
                return pe.matmul(dst, hi, xl, start=False, stop=True)

            def up1(n, e):
                k, behind = two_banks(n, e), is_last(n)
                if e == 0:
                    pe.wait_ge(x2l_ready, n + 1)
                if e > behind:
                    pe.wait_ge(sl_ready, ALL_E * n + e - behind)
                product(A1s[k][:], W1h[:, e, :], W1l[:, e, :], x2h[:], x2l[:]).then_inc(a1_mm, 1)

            def up3(n, e):
                k, behind = two_banks(n, e), is_last(n)
                if e > behind:
                    pe.wait_ge(h_ready, ALL_E * n + e - behind)
                product(A3s[k][:], W3h[:, e, :], W3l[:, e, :], x2h[:], x2l[:]).then_inc(a3_mm, 1)

            def down(n, e):
                k, behind = two_banks(n, e), is_last(n)
                pe.wait_ge(h_ready, ALL_E * n + e + 1)
                if e > behind:
                    pe.wait_ge(y_scaled, ALL_E * n + e - behind)
                for t in range(PAIRS):
                    last = pe.matmul(Ys[k][:, t * D:(t + 1) * D], h[:, e % 2, t * D:(t + 1) * D], W2[:, e, :],
                                     start=True, stop=True)
                last.then_inc(y_mm, 1)

            def middle(n, m, c):
                scores(n, 3)
                up1(m, 0)
                shift(n, 2)
                route(m)
                up3(m, 0)
                project_out(n, 0)
                scores(n, 4)
                shift(n, 3)
                up3(m, 1)
                up1(m, 1)
                down(m, 0)
                attention(n, 1)
                up1(m, 2)
                scores(n, 5)
                shift(n, 4)
                up3(m, 2)
                down(m, 1)
                up1(m, 3)
                scores(n, 6)
                project_out(n, 1)
                if c is not None:
                    turn_x(c)
                shift(n, 5)
                up3(m, 3)
                if c is not None:
                    queries(c)
                down(m, 2)
                attention(n, 2)
                scores(n, 7)
                up1(m, 4)
                up3(m, 4)

            def ends(n, m, c):
                down(m, 3)
                shift(n, 6)
                project_out(n, 2)
                if c is not None:
                    keys_values(c, 0)
                shift(n, 7)
                up1(m, 5)
                up3(m, 5)
                down(m, 4)
                if c is not None:
                    scores(c, 0)
                attention(n, 3)
                up1(m, 6)
                up3(m, 6)
                if c is not None:
                    scores(c, 1)
                down(m, 5)
                project_out(n, 3)
                up1(m, 7)
                if c is not None:
                    keys_values(c, 1)
                    shift(c, 0)
                up3(m, 7)
                down(m, 6)
                up1(m, 8)
                if c is not None:
                    scores(c, 2)
                up3(m, 8)
                if c is not None:
                    shift(c, 1)
                down(m, 7)
                if c is not None:
                    attention(c, 0)
                down(m, 8)
                turn_x2(n)

            pe.wait_ge(proj_loaded, 16)
            keys_values(0, 0, A1)
            keys_values(0, 1, A3)
            pe.wait_ge(rest_loaded, 32)
            pe.wait_ge(xn_first, 1)
            for t in range(2):
                last = pe.transpose(M0[:, t * D:(t + 1) * D], xn[:, t, :], ident)
            last.then_inc(xT_first_mm, 1)
            pe.wait_ge(set_dve, 3)
            pe.matmul(M1[:, 0:D], bv_rep[:], wo, start=True, stop=True).then_inc(bias_mm, 1)
            pe.wait_ge(xT_first, 1)
            pe.matmul(Y[:, 0:HALF], wq, xnT[:, 0:HALF], start=True, stop=True).then_inc(q_first_mm, 1)
            pe.wait_ge(xn_ready, 1)
            for t in range(2, PAIRS):
                last = pe.transpose(M0[:, t * D:(t + 1) * D], xn[:, t, :], ident)
            last.then_inc(xT_mm, 1)
            pe.wait_ge(xT_ready, 1)
            pe.wait_ge(q_first, 1)
            pe.matmul(Y[:, HALF:], wq, xnT[:, HALF:], start=True, stop=True).then_inc(q_mm, 1)
            scores(0, 0)
            scores(0, 1)
            pe.wait_ge(set_dve, 5)
            pe.wait_ge(rw_split, 1)
            pe.wait_ge(bias_ready, 1)
            pe.wait_ge(v_ready, 1)
            pe.wait_ge(q_ready, 1)
            scores(0, 2)
            shift(0, 0)
            scores(0, 3)
            shift(0, 1)
            scores(0, 4)
            shift(0, 2)
            attention(0, 0)
            shift(0, 3)
            scores(0, 5)
            shift(0, 4)
            project_out(0, 0)
            attention(0, 1)
            scores(0, 6)
            scores(0, 7)
            turn_x(1)
            project_out(0, 1)
            shift(0, 5)
            queries(1)
            shift(0, 6)
            keys_values(1, 0)
            attention(0, 2)
            shift(0, 7)
            scores(1, 0)
            attention(0, 3)
            project_out(0, 2)
            scores(1, 1)
            keys_values(1, 1)
            project_out(0, 3)
            shift(1, 0)
            scores(1, 2)
            shift(1, 1)
            attention(1, 0)
            turn_x2(0)
            pe.wait_ge(down_in, 16)
            pe.wait_ge(split_lo, 2)
            with pe.Fori(0, NCH - 2) as m:
                middle(m + 1, m, m + 2)
                ends(m + 1, m, m + 2)
            middle(NCH - 1, NCH - 2, None)
            ends(NCH - 1, NCH - 2, None)
            up1(NCH - 1, 0)
            route(NCH - 1)
            up3(NCH - 1, 0)
            up1(NCH - 1, 1)
            up1(NCH - 1, 2)
            down(NCH - 1, 0)
            up3(NCH - 1, 1)
            up3(NCH - 1, 2)
            up1(NCH - 1, 3)
            down(NCH - 1, 1)
            up1(NCH - 1, 4)
            up3(NCH - 1, 3)
            up3(NCH - 1, 4)
            down(NCH - 1, 2)
            down(NCH - 1, 3)
            up1(NCH - 1, 5)
            up1(NCH - 1, 6)
            up3(NCH - 1, 5)
            down(NCH - 1, 4)
            up1(NCH - 1, 7)
            up3(NCH - 1, 6)
            up1(NCH - 1, 8)
            down(NCH - 1, 5)
            up3(NCH - 1, 7)
            down(NCH - 1, 6)
            down(NCH - 1, 7)
            up3(NCH - 1, 8)
            down(NCH - 1, 8)


def kernel(x, ctx_1024, g_xattn, g_ffn, L0_xattn_Wq, L0_xattn_bq, L0_xattn_Wk, L0_xattn_bk, L0_xattn_Wv,
           L0_xattn_bv, L0_xattn_Wo, L0_xattn_bo, L0_ffn_router_w, L0_ffn_expert_bias, L0_ffn_w1, L0_ffn_w2,
           L0_ffn_w3, L0_ffn_sw1, L0_ffn_sw2, L0_ffn_sw3):
    import concourse.bacc as bacc
    from concourse.bass_utils import run_bass_kernel_spmd

    def arr(a):
        return np.ascontiguousarray(np.asarray(a))

    B, S, _ = x.shape
    woT = arr(L0_xattn_Wo).T
    wo_b = np.zeros((COLT, 2, 2, HD, 2, 2, D), woT.dtype)
    by_head = woT.reshape(COLT, 2, 2, HD, D)
    for b in range(2):
        wo_b[:, :, b, :, :, b, :] = by_head.transpose(0, 2, 3, 1, 4)

    def side_by_side(routed, shared):
        both = np.concatenate([arr(routed), arr(shared)[None]], axis=0)
        return arr(both.transpose(1, 0, 2)).reshape(D, ALL_E * D)

    ins = {
        "x": arr(x).reshape(B * S, D),
        "ctx_t": arr(arr(ctx_1024).reshape(B * S, D).T),
        "proj_w": arr(np.concatenate([arr(L0_xattn_Wk).T, arr(L0_xattn_Wv).T, arr(L0_xattn_Wq).T,
                                      np.stack([arr(L0_xattn_bq), arr(L0_xattn_bk), arr(L0_xattn_bv)], axis=1)],
                                     axis=1)),
        "rest_w": arr(np.concatenate([constants(), woT, wo_b.reshape(D, 4 * D), arr(L0_ffn_router_w)], axis=1)),
        "rows": arr(np.concatenate([arr(L0_xattn_bo), arr(L0_ffn_expert_bias), arr(g_xattn), arr(g_ffn)])),
        "w1": side_by_side(L0_ffn_w1, L0_ffn_sw1),
        "w2": side_by_side(L0_ffn_w2, L0_ffn_sw2),
        "w3": side_by_side(L0_ffn_w3, L0_ffn_sw3),
    }
    nc = bacc.Bacc("TRN2", target_bir_lowering=False, num_devices=1)
    aps = {n: nc.dram_tensor("in_" + n, a.shape, mybir.dt.from_np(a.dtype), kind="ExternalInput").ap()
           for n, a in ins.items()}
    out = nc.dram_tensor("out_y", (B * S, D), F32, kind="ExternalOutput").ap()
    block_program(nc, **aps, out=out)
    r = run_bass_kernel_spmd(nc, [{"in_" + n: a for n, a in ins.items()}], core_ids=[0])
    return r.results[0]["out_y"].reshape(B, S, D)
```
